# Optimizing a Trainium2 kernel written in Bass

```python
import numpy as np
import jax
import jax.numpy as jnp

def _softmax(x, axis=-1):
    return jax.nn.softmax(x, axis=axis)

def _gelu(x):
    return jax.nn.gelu(x, approximate=True)

def _silu(x):
    return jax.nn.silu(x)

def _sigmoid(x):
    return jax.nn.sigmoid(x)

def _layernorm(x, axis=-1, eps=1e-05):
    m = jnp.mean(x, axis=axis, keepdims=True)
    v = jnp.var(x, axis=axis, keepdims=True)
    return (x - m) / jnp.sqrt(v + eps)

def _scatter_add(tgt, idx, src, axis=0):
    return tgt.at[idx].add(src)

def _segment_sum(src, seg, n):
    return jax.ops.segment_sum(src, seg, n)
kernel_name = 'mk_gnn_preln_d2_gnn_r8_bbd753'

def setup_inputs(seed: int=0):
    np.random.seed(seed)
    _w = jnp.asarray

    def _rec_inputs():
        import jax
        import jax.numpy as jnp
        _gk = jax.random.key(seed)
        x = -0.0006008 + 1.001 * jax.random.normal(jax.random.fold_in(_gk, 1), (12500, 128), jnp.float32)
        _s = jax.random.randint(jax.random.fold_in(_gk, 2), (100000,), 0, 12500, jnp.int32)
        _d = jax.random.randint(jax.random.fold_in(_gk, 3), (100000,), 0, 12500, jnp.int32)
        _loop = jnp.arange(12500, dtype=jnp.int32)
        src = jnp.concatenate([_s, _d, _loop])
        dst = jnp.concatenate([_d, _s, _loop])
        _o = jnp.argsort(dst, stable=True)
        src = src[_o]
        dst = dst[_o]
        edge_attr_20 = jax.random.uniform(jax.random.fold_in(_gk, 12), (212500, 20), jnp.float32, 0.0, 1)
        edge_type_16 = jax.random.randint(jax.random.fold_in(_gk, 14), (212500,), 0, 16, jnp.int32)
        edge_weight = jax.random.uniform(jax.random.fold_in(_gk, 15), (212500,), jnp.float32, 0.0, 0.999998)
        return (x, src, dst, edge_attr_20, edge_type_16, edge_weight)
    x, src, dst, edge_attr_20, edge_type_16, edge_weight = _rec_inputs()

    def _L0_gnn_setup():
        import jax, jax.numpy as jnp
        import numpy as np
        N_ATOMS = 2500
        N_EDGES = 80000
        N_BASIS = 128
        N_RBF = 20
        N_FILT = 128

        def ssp(v):
            return jax.nn.softplus(v) - jnp.log(2.0).astype(v.dtype)
        key = jax.random.key(seed)
        ks = jax.random.split(key, 16)
        s = lambda fan_in: 1.0 / np.sqrt(fan_in)
        return {'x': jax.random.normal(ks[0], (N_ATOMS, N_BASIS), dtype=jnp.float32), 'f_ij': jax.random.uniform(ks[1], (N_EDGES, N_RBF), dtype=jnp.float32), 'rcut_ij': jax.random.uniform(ks[2], (N_EDGES,), dtype=jnp.float32), 'idx_i': jax.random.randint(ks[3], (N_EDGES,), 0, N_ATOMS), 'idx_j': jax.random.randint(ks[4], (N_EDGES,), 0, N_ATOMS), 'W_in2f': jax.random.normal(ks[5], (N_BASIS, N_FILT), dtype=jnp.float32) * s(N_BASIS), 'W_filt1': jax.random.normal(ks[6], (N_RBF, N_FILT), dtype=jnp.float32) * s(N_RBF), 'b_filt1': jnp.zeros((N_FILT,), dtype=jnp.float32), 'W_filt2': jax.random.normal(ks[7], (N_FILT, N_FILT), dtype=jnp.float32) * s(N_FILT), 'b_filt2': jnp.zeros((N_FILT,), dtype=jnp.float32), 'W_out1': jax.random.normal(ks[8], (N_FILT, N_BASIS), dtype=jnp.float32) * s(N_FILT), 'b_out1': jnp.zeros((N_BASIS,), dtype=jnp.float32), 'W_out2': jax.random.normal(ks[9], (N_BASIS, N_BASIS), dtype=jnp.float32) * s(N_BASIS), 'b_out2': jnp.zeros((N_BASIS,), dtype=jnp.float32)}
    _L0_gnn_all = _L0_gnn_setup()
    _L0_gnn_in = {k: v for k, v in _L0_gnn_all.items() if k in ('W_in2f', 'W_filt1', 'b_filt1', 'W_filt2', 'b_filt2', 'W_out1', 'b_out1', 'W_out2', 'b_out2')}
    del _L0_gnn_all

    def _L1_gnn_setup():
        import jax, jax.numpy as jnp
        import numpy as np
        NUM_NODES = 6250
        NUM_RELATIONS = 16
        HIDDEN = 128
        NUM_LAYERS = 3
        NUM_EDGES = 200000

        def _fast_rgcn_layer(x, src, tgt, edge_type, W_r, root_r, bias_r):
            N, d = x.shape
            R = W_r.shape[0]
            seg = tgt * R + edge_type
            msg = x[src]
            agg = jax.ops.segment_sum(msg, seg, num_segments=N * R).reshape(N, R, d)
            cnt = jax.ops.segment_sum(jnp.ones_like(edge_type, dtype=x.dtype), seg, num_segments=N * R).reshape(N, R, 1)
            agg = agg / jnp.clip(cnt, 1.0, None)
            out = jnp.einsum('nrd,rdo->no', agg, W_r)
            out = out + x @ root_r + bias_r
            return out
        key = jax.random.key(seed)
        ks = jax.random.split(key, 6)
        edge_index = jax.random.randint(ks[0], (2, NUM_EDGES), 0, NUM_NODES, dtype=jnp.int64)
        edge_type = jax.random.randint(ks[1], (NUM_EDGES,), 0, NUM_RELATIONS, dtype=jnp.int64)
        scale = 1.0 / np.sqrt(HIDDEN)
        node_init = jax.random.normal(ks[2], (NUM_NODES, HIDDEN), dtype=jnp.float32) * scale
        W = jax.random.normal(ks[3], (NUM_LAYERS, NUM_RELATIONS, HIDDEN, HIDDEN), dtype=jnp.float32) * scale
        root = jax.random.normal(ks[4], (NUM_LAYERS, HIDDEN, HIDDEN), dtype=jnp.float32) * scale
        bias = jnp.zeros((NUM_LAYERS, HIDDEN), dtype=jnp.float32)
        return {'edge_index': edge_index, 'edge_type': edge_type, 'node_init': node_init, 'W': W, 'root': root, 'bias': bias}
    _L1_gnn_all = _L1_gnn_setup()
    _L1_gnn_in = {k: v for k, v in _L1_gnn_all.items() if k in ('W', 'root', 'bias')}
    del _L1_gnn_all
    return {'x': x, 'src': src, 'dst': dst, 'edge_attr_20': edge_attr_20, 'edge_type_16': edge_type_16, 'edge_weight': edge_weight, 'L0_gnn_W_in2f': _L0_gnn_in['W_in2f'], 'L0_gnn_W_filt1': _L0_gnn_in['W_filt1'], 'L0_gnn_b_filt1': _L0_gnn_in['b_filt1'], 'L0_gnn_W_filt2': _L0_gnn_in['W_filt2'], 'L0_gnn_b_filt2': _L0_gnn_in['b_filt2'], 'L0_gnn_W_out1': _L0_gnn_in['W_out1'], 'L0_gnn_b_out1': _L0_gnn_in['b_out1'], 'L0_gnn_W_out2': _L0_gnn_in['W_out2'], 'L0_gnn_b_out2': _L0_gnn_in['b_out2'], 'L1_gnn_W': _L1_gnn_in['W'], 'L1_gnn_root': _L1_gnn_in['root'], 'L1_gnn_bias': _L1_gnn_in['bias']}

def reference(x, src, dst, edge_attr_20, edge_type_16, edge_weight, L0_gnn_W_in2f, L0_gnn_W_filt1, L0_gnn_b_filt1, L0_gnn_W_filt2, L0_gnn_b_filt2, L0_gnn_W_out1, L0_gnn_b_out1, L0_gnn_W_out2, L0_gnn_b_out2, L1_gnn_W, L1_gnn_root, L1_gnn_bias):
    import jax
    import jax.numpy as jnp

    def _L0_gnn_ref(x, f_ij, rcut_ij, idx_i, idx_j, W_in2f, W_filt1, b_filt1, W_filt2, b_filt2, W_out1, b_out1, W_out2, b_out2):
        import jax, jax.numpy as jnp
        import numpy as np
        N_ATOMS = 2500
        N_EDGES = 80000
        N_BASIS = 128
        N_RBF = 20
        N_FILT = 128

        def ssp(v):
            return jax.nn.softplus(v) - jnp.log(2.0).astype(v.dtype)
        n_atoms = x.shape[0]
        h = x @ W_in2f
        Wij = ssp(f_ij @ W_filt1 + b_filt1) @ W_filt2 + b_filt2
        Wij = Wij * rcut_ij[:, None]
        x_ij = h[idx_j] * Wij
        agg = jax.ops.segment_sum(x_ij, idx_i, num_segments=n_atoms)
        out = ssp(agg @ W_out1 + b_out1) @ W_out2 + b_out2
        return out

    def _L1_gnn_ref(edge_index, edge_type, node_init, W, root, bias):
        import jax, jax.numpy as jnp
        import numpy as np
        NUM_NODES = 6250
        NUM_RELATIONS = 16
        HIDDEN = 128
        NUM_LAYERS = 3
        NUM_EDGES = 200000

        def _fast_rgcn_layer(x, src, tgt, edge_type, W_r, root_r, bias_r):
            N, d = x.shape
            R = W_r.shape[0]
            seg = tgt * R + edge_type
            msg = x[src]
            agg = jax.ops.segment_sum(msg, seg, num_segments=N * R).reshape(N, R, d)
            cnt = jax.ops.segment_sum(jnp.ones_like(edge_type, dtype=x.dtype), seg, num_segments=N * R).reshape(N, R, 1)
            agg = agg / jnp.clip(cnt, 1.0, None)
            out = jnp.einsum('nrd,rdo->no', agg, W_r)
            out = out + x @ root_r + bias_r
            return out
        src, tgt = (edge_index[0], edge_index[1])
        x = node_init
        for i in range(NUM_LAYERS):
            x = _fast_rgcn_layer(x, src, tgt, edge_type, W[i], root[i], bias[i])
            if i < NUM_LAYERS - 1:
                x = jax.nn.relu(x)
        return x
    edge_index = jnp.stack([src, dst])
    h = jnp.maximum(_layernorm(x, axis=-1), 0.0)
    x = x + _L0_gnn_ref(h, edge_attr_20, edge_weight, src, dst, L0_gnn_W_in2f, L0_gnn_W_filt1, L0_gnn_b_filt1, L0_gnn_W_filt2, L0_gnn_b_filt2, L0_gnn_W_out1, L0_gnn_b_out1, L0_gnn_W_out2, L0_gnn_b_out2)
    h = jnp.maximum(_layernorm(x, axis=-1), 0.0)
    x = x + _L1_gnn_ref(edge_index, edge_type_16, h, L1_gnn_W, L1_gnn_root, L1_gnn_bias)
    return x

_drawn_inputs = setup_inputs


def setup_inputs(seed=0):
    import zlib

    import numpy as np

    out = dict(_drawn_inputs(seed))
    spreads = {'L0_gnn_b_filt1': (0.0, 0.1),
     'L0_gnn_b_filt2': (0.0, 0.1),
     'L0_gnn_b_out1': (0.0, 0.1),
     'L0_gnn_b_out2': (0.0, 0.1),
     'L1_gnn_bias': (0.0, 0.1)}
    factors = {}
    for name, (base, spread) in spreads.items():
        noise = np.random.default_rng([zlib.crc32(name.encode()), seed]).standard_normal(out[name].shape)
        drawn = base * np.exp(spread * noise) if base else spread * noise
        out[name] = jnp.asarray(drawn.astype(out[name].dtype))
    for name, factor in factors.items():
        out[name] = (out[name] * factor).astype(out[name].dtype)
    return out
```

```python
from contextlib import ExitStack

import concourse.bass as bass
from concourse import mybir

P = 128
G = 4
R = 16
NRBF = 20
REC = NRBF + 5
CUT, DST, ROW, SBLK, SRC = range(NRBF, REC)
MSG = P + 1
AHEAD = float(1 << 18)
EPS = 1e-5

ALU = mybir.AluOpType
ACT = mybir.ActivationFunctionType
AX = mybir.AxisListType.X
F32 = mybir.dt.float32
BF16 = mybir.dt.bfloat16
I32 = mybir.dt.int32


def ceil_to(n, m):
    return (n + m - 1) // m * m


def gnn_kernel(nc, x, src, dst, edge_attr, edge_type, edge_weight, w_in, w_f1, b_f1, w_f2, b_f2,
               w_o1, b_o1, w_o2, b_o2, w_rel, w_root, bias_rel, out):
    N = x.shape[0]
    E = src.shape[0]
    LAYERS = w_rel.shape[0]
    NB = -(-N // P)
    NBP = ceil_to(NB, G)
    TE = ceil_to(-(-E // P), 2 * G)
    T = ceil_to((E + (P - 1) * NB) // P, 2 * G)
    NG = TE // G
    FULL = E // (G * P)
    REST = E - FULL * G * P
    CHUNKS = next(d for d in range(-(-NG // P), NG + 1) if NG % d == 0)
    CR = NG // CHUNKS
    HALF_E, HALF_T = TE // (2 * G), T // (2 * G)
    LAST = N - (NB - 1) * P
    CH = 440 if T % 440 == 0 else T // 4
    assert NB * G <= 512 and T % CH == 0 and CH <= 512 and E + P < AHEAD
    assert REST % G == 0 and REST > 0 and FULL == NG - 1

    def dram(name, shape, dt=F32):
        return nc.dram_tensor(name, shape, dt).ap()

    recs = dram("edges_by_dst_block", [E + P, REC])
    msgs = dram("messages_by_src_block", [E + P, MSG])
    xpad = dram("x_padded", [NBP * P, P])
    x1d = dram("x_after_layer0", [NBP * P, P])
    ytab = dram("relation_products", [NB * P, R * P])
    yrows = ytab.rearrange("n (r f) -> (n r) f", r=R)

    def wait(e, s, value):
        if not isinstance(value, int) or value > 0:
            e.wait_ge(s, value)

    def halves(e, count, group, peel_last=False):
        for h in range(2):
            group(0, h)
        with e.Fori(1, count - peel_last) as i:
            for h in range(2):
                group(i, h)
        if peel_last:
            for h in range(2):
                group(count - 1, h)

    def staggered(e, count, first, second):
        first(0, 0)
        first(0, 1)
        second(0, 0)
        with e.Fori(1, count) as i:
            first(i, 0)
            second(i - 1, 1)
            first(i, 1)
            second(i, 0)
        second(count - 1, 1)

    taken = {}

    def unique(name):
        taken[name] = taken.get(name, 0) + 1
        return name if taken[name] == 1 else f"{name}_{taken[name]}"

    ctx = ExitStack()
    with ctx:
        def sb(name, shape, dt=F32, c=ctx):
            return c.enter_context(nc.sbuf_tensor(unique(name), shape, dt))

        def psum(name, shape, dt=F32, c=ctx):
            return c.enter_context(nc.psum_tensor(unique(name), shape, dt))

        def sem(name, c=ctx):
            return c.enter_context(nc.semaphore(unique(name)))

        iota = sb("iota", [P, 160])
        identf = sb("identf", [P, P])
        identb = sb("identb", [P, P], BF16)
        onesf = sb("onesf", [P, P])
        onesb = sb("onesb", [P, P], BF16)
        before = sb("before", [P, P], BF16)
        notbefore = sb("notbefore", [P, P], BF16)
        maps = sb("maps", [P, T], I32)
        blk_d = sb("blk_d", [P, T])
        blk_s = sb("blk_s", [P, T])
        starts = sb("starts", [P, 2, NB])
        loc = sb("loc", [P, T])
        row = sb("row", [P, T])
        typ = sb("typ", [P, T])
        counts = sb("counts", [P, NB * R])
        wgt = sb("wgt", [P, T])
        s_passed = {eng.engine: sem(f"passed_{n}") for n, eng in
                    enumerate((nc.vector, nc.scalar, nc.tensor, nc.gpsimd))}

        def settle(e):
            e.sem_inc(s_passed[e.engine], 1)

        def tile_values(e, lane, first, most):
            _, values = nc.values_load_multi_w_load_instructions(
                maps[lane:lane + 1, bass.ds(first, G)], engines=[e.engine], min_val=0, max_val=most,
                skip_runtime_bounds_check_because="the tile maps are clamped to this range")
            return values

        def over_groups(ap, width):
            return ap.unsqueeze(1).broadcast_to([ap.shape[0], G, width])

        def over_width(ap, width):
            return ap.unsqueeze(2).broadcast_to([ap.shape[0], G, width])


        sorting = ExitStack()
        aux = sb("aux", [P, TE, REC - NRBF], c=sorting)
        dkey = sb("dkey", [P, TE], c=sorting)
        skey = sb("skey", [P, TE], c=sorting)
        with ExitStack() as c:
            kint = sb("kint", [CR, 3, CHUNKS, G * P], I32, c)
            bint = sb("bint", [CR, CHUNKS, G * P], I32, c)
            fld = sb("fld", [CR, 6, CHUNKS, G * P], c=c)
            cnt = sb("cnt", [P, 2, NB], c=c)
            num = sb("num", [P, 2, NB + 1], c=c)
            numi = sb("numi", [P, 2, NB + 1], I32, c)
            til = sb("til", [P, 2, NB + 1], c=c)
            zero = sb("zero", [P, NB], c=c)
            tend = sb("tend", [P, 2, NB], c=c)
            nend = sb("nend", [P, 2, NB], c=c)
            tcol = sb("tcol", [P, 2], c=c)
            slack = sb("slack", [P, 2], c=c)
            slackb = sb("slackb", [P, 2, P], BF16, c)
            iotat = sb("iotat", [P, T], c=c)
            past = sb("past", [P, 2, T], BF16, c)
            junk = past[:, :, 0:TE]
            ps_row = psum("ps_row", [P, 2, NB], c=c)
            ps_col = psum("ps_col", [P, 4], c=c)
            ps_b = psum("ps_b", [P, CH], c=c)
            ps_o = psum("ps_o", [P, CH], c=c)
            offs = sb("offs", [P, CH], c=c)
            s_pad, s_in, s_pool, s_v = sem("pads_set", c), sem("keys_loaded", c), sem("pool_consts", c), sem("dve_step", c)
            s_cnt, s_num, s_tend, s_tcol = sem("counted", c), sem("numbers", c), sem("tile_ends", c), sem("tile_ends_col", c)
            s_past, s_map, s_mapd = sem("past_ready", c), sem("map_products", c), sem("map_done", c)
            s_fld, s_tr, s_ev = sem("fields_ready", c), sem("fields_turned", c), sem("fields_copied", c)
            ps_t = psum("ps_t", [P, 2, 512], c=c)
            with nc.Block() as block:

                @block.sync
                def _(e):
                    e.wait_ge(s_pad, 2)
                    for n, a in enumerate((dst, src, edge_type, edge_weight)):
                        to = kint[:, n] if n < 3 else fld[:, CUT - NRBF]
                        full = a[0:FULL * G * P].rearrange("(c q) -> c q", q=G * P)
                        for ch in range(CHUNKS):
                            rows = min(CR, FULL - ch * CR)
                            e.dma_start(to[0:rows, ch, :], full[ch * CR:ch * CR + rows, :]).then_inc(s_in, 16)
                        e.dma_start(to[CR - 1:CR, CHUNKS - 1, 0:REST],
                                    a[FULL * G * P:E].rearrange("(p t) -> p t", p=1)).then_inc(s_in, 16)

                @block.gpsimd
                def _(e):
                    e.iota(iota[:, :], [[1, 160]], base=0, channel_multiplier=0,
                           allow_small_or_imprecise_dtypes=True).then_inc(s_pool, 1)
                    e.iota(iotat[:, :], [[1, T]], base=0, channel_multiplier=0,
                           allow_small_or_imprecise_dtypes=True).then_inc(s_pool, 1)
                    e.memset(identf[:, :], 0.0).then_inc(s_pool, 1)
                    e.memset(onesf[:, :], 1.0).then_inc(s_pool, 1)
                    e.memset(onesb[:, :], 1.0).then_inc(s_pool, 1)
                    e.wait_ge(s_pool, 5)
                    e.affine_select(out=identf[:, :], in_=identf[:, :], compare_op=ALU.not_equal, fill=1.0,
                                    base=0, pattern=[[-1, P]], channel_multiplier=1).then_inc(s_pool, 1)
                    e.affine_select(out=before[:, :], in_=onesb[:, :], compare_op=ALU.is_gt, fill=0.0,
                                    base=0, pattern=[[1, P]], channel_multiplier=-1).then_inc(s_pool, 1)
                    e.affine_select(out=notbefore[:, :], in_=onesb[:, :], compare_op=ALU.is_ge, fill=0.0,
                                    base=0, pattern=[[-1, P]], channel_multiplier=1).then_inc(s_pool, 1)

                @block.vector
                def _(e):
                    steps = [0]

                    def then_wait(ins):
                        steps[0] += 1
                        ins.then_inc(s_v, 1)
                        e.wait_ge(s_v, steps[0])

                    e.memset(kint[:, :, :, :], -1).then_inc(s_pad, 1)
                    e.memset(fld[:, CUT - NRBF, :, :], 0.0).then_inc(s_pad, 1)
                    e.memset(zero[:, :], 0.0)
                    then_wait(e.memset(num[:, :, :], 0.0))
                    e.wait_ge(s_pool, 8)
                    e.tensor_copy(identb[:, :], identf[:, :])
                    e.wait_ge(s_in, 16 * 4 * (CHUNKS + 1))
                    then_wait(e.tensor_scalar(bint[:, :, :], kint[:, 1], 7, None, ALU.arith_shift_right))
                    then_wait(e.tensor_scalar(fld[:, SBLK - NRBF], bint[:, :, :], 1.0, None, ALU.add))
                    then_wait(e.tensor_scalar(bint[:, :, :], kint[:, 0], 7, None, ALU.arith_shift_right))
                    e.tensor_copy(fld[:, 5], bint[:, :, :])
                    e.tensor_copy(fld[:, DST - NRBF], kint[:, 0])
                    e.tensor_copy(fld[:, SRC - NRBF], kint[:, 1])
                    e.scalar_tensor_tensor(out=fld[:, ROW - NRBF], in0=kint[:, 1], scalar=float(R),
                                           in1=kint[:, 2], op0=ALU.mult, op1=ALU.add).then_inc(s_fld, 1)
                    done = 0
                    for f in range(6):
                        for ch in range(CHUNKS):
                            done += 1
                            e.wait_ge(s_tr, done)
                            turned = ps_t[:, done % 2, 0:G * CR].rearrange("p (k c) -> p c k", k=G)
                            if f < 5:
                                e.tensor_copy(aux[:, ch * CR * G:(ch + 1) * CR * G, f].rearrange("p (c k) -> p c k", k=G),
                                              turned).then_inc(s_ev, 1)
                            else:
                                e.tensor_copy(dkey[:, ch * CR * G:(ch + 1) * CR * G].rearrange("p (c k) -> p c k", k=G),
                                              turned).then_inc(s_ev, 1)
                    e.wait_ge(s_ev, done)
                    then_wait(e.tensor_copy(skey[:, :], aux[:, :, SBLK - NRBF]))
                    for b in range(NB):
                        wait(e, s_cnt, 2 * b - 1)
                        e.tensor_scalar(junk[:, 0], dkey[:, :], float(b), None, ALU.is_equal, ALU.add,
                                        accum_out=cnt[:, 0, b:b + 1]).then_inc(s_cnt, 1)
                        wait(e, s_cnt, 2 * b)
                        e.tensor_scalar(junk[:, 1], skey[:, :], float(b + 1), None, ALU.is_equal, ALU.add,
                                        accum_out=cnt[:, 1, b:b + 1]).then_inc(s_cnt, 1)
                    e.wait_ge(s_num, 1)
                    e.tensor_copy(num[:, :, 0:NB], ps_row[:, :, :])
                    then_wait(e.tensor_copy(num[0:NB, :, NB], ps_col[0:NB, 0:2]))
                    then_wait(e.tensor_scalar(numi[:, :, :], num[:, :, :], float(P - 1), None, ALU.add))
                    then_wait(e.tensor_scalar(numi[:, :, :], numi[:, :, :], 7, None, ALU.arith_shift_right))
                    then_wait(e.tensor_copy(til[:, :, :], numi[:, :, :]))
                    for n in range(2):
                        e.tensor_tensor_scan(tend[:, n, :], til[:, n, 0:NB], zero[:, :], 0.0, ALU.add, ALU.add)
                        then_wait(e.tensor_tensor_scan(nend[:, n, :], num[:, n, 0:NB], zero[:, :], 0.0,
                                                       ALU.add, ALU.add))
                    then_wait(e.tensor_tensor(starts[:, :, :], nend[:, :, :], num[:, :, 0:NB], ALU.subtract))
                    e.tensor_scalar(starts[:, :, :], starts[:, :, :], -AHEAD, None, ALU.add)
                    then_wait(e.scalar_tensor_tensor(out=slack[:, :], in0=til[:, :, NB], scalar=-float(P),
                                                     in1=num[:, :, NB], op0=ALU.mult, op1=ALU.add))
                    for n in range(2):
                        ins = e.tensor_scalar(slackb[:, n, :], onesb[:, :], slack[:, n:n + 1], None, ALU.mult)
                    ins.then_inc(s_tend, 1)
                    e.wait_ge(s_tcol, 1)
                    then_wait(e.tensor_copy(tcol[0:NB, :], ps_col[0:NB, 2:4]))
                    for n in range(2):
                        ins = e.tensor_scalar(past[0:NB, n, :], iotat[0:NB, :], tcol[0:NB, n:n + 1], None, ALU.is_ge)
                    ins.then_inc(s_past, 1)
                    done = 0
                    for n in range(2):
                        blk = (blk_d, blk_s)[n]
                        for q in range(0, T, CH):
                            done += 1
                            e.wait_ge(s_map, done)
                            e.tensor_scalar(blk[:, q:q + CH], ps_b[:, :], float(NB - 1), float(P), ALU.min, ALU.mult)
                            e.tensor_scalar(maps[64 * n:64 * n + 32, q:q + CH], ps_b[64 * n:64 * n + 32, :],
                                            float(NB - 1), float(R), ALU.min, ALU.mult)
                            then_wait(e.scalar_tensor_tensor(out=offs[:, :], in0=iotat[:, q:q + CH], scalar=float(P),
                                                             in1=ps_o[:, :], op0=ALU.mult, op1=ALU.add))
                            lane = 64 * n + 32
                            e.tensor_scalar(maps[lane:lane + 32, q:q + CH], offs[lane:lane + 32, :],
                                            float(E), None, ALU.min).then_inc(s_mapd, 1)
                            e.wait_ge(s_mapd, done)

                @block.tensor
                def _(e):
                    e.wait_ge(s_fld, 1)
                    e.wait_ge(s_pool, 8)
                    done = 0
                    for f in range(6):
                        for ch in range(CHUNKS):
                            done += 1
                            wait(e, s_ev, done - 2)
                            lanes = fld[:, f, ch, :].rearrange("c (p k) -> c k p", k=G)
                            for k in range(G):
                                mm = e.transpose(ps_t[:, done % 2, k * CR:(k + 1) * CR], lanes[:, k, :],
                                                 identf[0:CR, 0:CR])
                            mm.then_inc(s_tr, 1)
                    e.wait_ge(s_cnt, 2 * NB)
                    for n in range(2):
                        e.matmul(ps_row[:, n, :], onesf[:, :], cnt[:, n, :], start=True, stop=True)
                        mm = e.matmul(ps_col[0:NB, n:n + 1], cnt[:, n, :], onesf[:, 0:1], start=True, stop=True)
                    mm.then_inc(s_num, 1)
                    e.wait_ge(s_tend, 1)
                    for n in range(2):
                        mm = e.matmul(ps_col[0:NB, 2 + n:3 + n], tend[0:1, n, :], onesf[0:1, 0:1], start=True, stop=True)
                    mm.then_inc(s_tcol, 1)
                    e.wait_ge(s_past, 1)
                    done = 0
                    for n in range(2):
                        for q in range(0, T, CH):
                            wait(e, s_mapd, done)
                            e.matmul(ps_b[:, :], onesb[0:NB, :], past[0:NB, n, q:q + CH], start=True, stop=True)
                            e.matmul(ps_o[:, :], slackb[0:NB, n, :], past[0:NB, n, q:q + CH], start=True, stop=True)\
                             .then_inc(s_map, 1)
                            done += 1

        def rank_start(e, ranks, n):
            e.matmul(ranks[:, :, :], onesf[0:1, :], over_groups(starts[0:1, n, :], NB), start=True, stop=True,
                     skip_group_check=True)

        def rank_before(e, ranks, hot):
            mm = e.matmul(ranks[:, :, :], before[:, :], hot[:, :, :], start=False, stop=True, skip_group_check=True)
            for j in range(G - 1):
                mm = e.matmul(ranks[:, j + 1:G, :], onesb[:, :],
                              hot[:, j:j + 1, :].broadcast_to([P, G - 1 - j, NB]),
                              start=False, stop=True, skip_group_check=True)
            return mm

        def rank_after(e, ranks, hot):
            mm = e.matmul(ranks[:, :, :], notbefore[:, :], hot[:, :, :], start=False, stop=True,
                          skip_group_check=True)
            for j in range(1, G):
                mm = e.matmul(ranks[:, 0:j, :], onesb[:, :], hot[:, j:j + 1, :].broadcast_to([P, j, NB]),
                              start=False, stop=True, skip_group_check=True)
            return mm

        with sorting, ExitStack() as c:
            hot = [sb(f"hot{h}", [P, G, NB], BF16, c) for h in range(2)]
            rank = sb("rank", [P, G, NB], c=c)
            posf = [sb(f"posf{h}", [P, G], c=c) for h in range(2)]
            pos = [sb(f"pos{h}", [P, G], I32, c) for h in range(2)]
            fin = [sb(f"fin{h}", [P, G, NRBF], c=c) for h in range(2)]
            rec = [sb(f"rec{h}", [P, G, REC], c=c) for h in range(2)]
            tail = sb("tail", [P, MSG], c=c)
            ranks = psum("ranks", [P, G, NB], c=c)
            s_f = [sem(f"basis_loaded{h}", c) for h in range(2)]
            s_sc = [sem(f"records_stored{h}", c) for h in range(2)]
            s_rec, s_hot, s_before, s_read = sem("records_built", c), sem("hot_built", c), sem("ranks_ready", c), sem("ranks_read", c)
            s_red, s_pos, s_after = sem("ranks_summed", c), sem("positions_ready", c), sem("ranks_moved", c)
            s_tail, s_tout = sem("tail_set", c), sem("tail_stored", c)
            with nc.Block() as block:

                @block.sync
                def _(e):
                    e.wait_ge(s_tail, 1)
                    e.dma_start(recs[E:E + P, :], tail[:, 0:REC]).then_inc(s_tout, 16)
                    e.dma_start(msgs[E:E + P, :], tail[:, :]).then_inc(s_tout, 16)

                    def group(i, h):
                        wait(e, s_rec, 2 * (2 * i + h - 1))
                        lanes = REST // G if isinstance(i, int) and 2 * i + h == NG - 1 else P
                        e.dma_start(fin[h][0:lanes, :, :],
                                    edge_attr[bass.ds((2 * i + h) * (G * P), lanes * G), :]
                                    .rearrange("(p k) f -> p k f", k=G)).then_inc(s_f[h], 16)

                    halves(e, HALF_E, group, peel_last=True)
                    e.wait_ge(s_tout, 32)

                @block.vector
                def _(e):
                    e.memset(tail[:, :], -1.0).then_inc(s_tail, 1)

                    def group(i, h):
                        g = 2 * i + h
                        wait(e, s_after, g - 1)
                        e.tensor_tensor(hot[h][:, :, :], over_groups(iota[:, 0:NB], NB),
                                        over_width(dkey[:, bass.ds(g * G, G)], NB), ALU.is_equal).then_inc(s_hot, 1)
                        wait(e, s_red, g)
                        e.wait_ge(s_before, g + 1)
                        e.tensor_tensor(rank[:, :, :], ranks[:, :, :], hot[h][:, :, :], ALU.mult).then_inc(s_read, 1)
                        e.wait_ge(s_read, g + 1)
                        e.tensor_reduce(posf[h][:, :], rank[:, :, :], AX, ALU.add).then_inc(s_red, 1)
                        e.wait_ge(s_red, g + 1)
                        wait(e, s_sc[h], i * (16 * G))
                        e.tensor_scalar(pos[h][:, :], posf[h][:, :], AHEAD, None, ALU.add).then_inc(s_pos, 1)

                    halves(e, HALF_E, group)

                @block.tensor
                def _(e):
                    rank_start(e, ranks, 0)

                    def group(i, h):
                        g = 2 * i + h
                        e.wait_ge(s_hot, g + 1)
                        rank_before(e, ranks, hot[h]).then_inc(s_before, 1)
                        e.wait_ge(s_read, g + 1)
                        rank_after(e, ranks, hot[h]).then_inc(s_after, 1)

                    halves(e, HALF_E, group)

                @block.scalar
                def _(e):
                    def group(i, h):
                        g = 2 * i + h
                        e.wait_ge(s_f[h], 16 * (i + 1))
                        wait(e, s_sc[h], i * (16 * G))
                        e.activation(rec[h][:, :, 0:NRBF], fin[h][:, :, :], ACT.Copy).then_inc(s_rec, 1)
                        e.activation(rec[h][:, :, NRBF:REC], aux[:, bass.ds(g * G, G), :], ACT.Copy).then_inc(s_rec, 1)

                    halves(e, HALF_E, group)

                @block.gpsimd
                def _(e):
                    def group(i, h):
                        g = 2 * i + h
                        e.wait_ge(s_rec, 2 * (g + 1))
                        e.wait_ge(s_pos, g + 1)
                        settle(e)
                        for k in range(G):
                            e.indirect_dma_start(
                                out=recs, out_offset=bass.IndirectOffsetOnAxis(ap=pos[h][:, k:k + 1], axis=0),
                                in_=rec[h][:, k, :], in_offset=None, bounds_check=E - 1, oob_is_err=False)\
                             .then_inc(s_sc[h], 16)

                    halves(e, HALF_E, group)
                    for h in range(2):
                        e.wait_ge(s_sc[h], HALF_E * 16 * G)

        messages = ExitStack()
        hf = sb("hf", [P, NB, 3, P], BF16, messages)
        with ExitStack() as c:
            xs = sb("xs", [P, NBP, P], c=c)
            mean = sb("mean", [P, NBP], c=c)
            var = sb("var", [P, NBP], c=c)
            std = sb("std", [P, NBP], c=c)
            rstd = sb("rstd", [P, NBP], c=c)
            win = sb("win", [P, P], c=c)
            sq = sb("sq", [P, G, P], c=c)
            hn = sb("hn", [P, G, P], c=c)
            hT = sb("hT", [P, G, P], c=c)
            left = sb("left", [P, G, P], c=c)
            ps_tr = psum("ps_tr", [P, G, P], c=c)
            ps_hf = psum("ps_hf", [P, G, P], c=c)
            s_in, s_set, s_out = sem("x_loaded", c), sem("x_pad_set", c), sem("x_stored", c)
            s_v, s_var, s_std = sem("dve_step", c), sem("variances_ready", c), sem("std_ready", c)
            s_hn, s_tr, s_hT, s_hf = sem("h_ready", c), sem("h_turned", c), sem("hT_ready", c), sem("hf_ready", c)
            s_hi, s_mid, s_lo = sem("high_part", c), sem("middle_part", c), sem("low_part", c)
            s_sub = sem("rest_ready", c)
            with nc.Block() as block:

                @block.sync
                def _(e):
                    e.dma_start(win[:, :], w_in).then_inc(s_in, 16)
                    e.wait_ge(s_set, 1)
                    e.dma_start(xs[:, 0:NB - 1, :], x[0:(NB - 1) * P, :].rearrange("(m p) f -> p m f", p=P)).then_inc(s_in, 16)
                    e.dma_start(xs[0:LAST, NB - 1, :], x[(NB - 1) * P:N, :]).then_inc(s_in, 16)
                    e.wait_ge(s_in, 48)
                    e.dma_start(xpad.rearrange("(m p) f -> p m f", p=P), xs[:, :, :]).then_inc(s_out, 16)
                    e.wait_ge(s_out, 16)

                def split(e, n):
                    m = min(G, NB - n * G)
                    part = hf[:, n * G:n * G + m, :, :]
                    e.wait_ge(s_hf, n + 1)
                    e.tensor_copy(part[:, :, 0, :], ps_hf[:, 0:m, :]).then_inc(s_hi, 1)
                    e.wait_ge(s_hi, n + 1)
                    e.tensor_tensor(left[:, 0:m, :], ps_hf[:, 0:m, :], part[:, :, 0, :], ALU.subtract).then_inc(s_sub, 1)
                    e.wait_ge(s_sub, n + 1)
                    e.tensor_copy(part[:, :, 1, :], left[:, 0:m, :]).then_inc(s_mid, 1)
                    e.wait_ge(s_mid, n + 1)
                    e.tensor_tensor(part[:, :, 2, :], left[:, 0:m, :], part[:, :, 1, :], ALU.subtract).then_inc(s_lo, 1)
                    e.wait_ge(s_lo, n + 1)

                @block.vector
                def _(e):
                    steps = [0]

                    def then_wait(ins):
                        steps[0] += 1
                        ins.then_inc(s_v, 1)
                        e.wait_ge(s_v, steps[0])

                    e.memset(xs[:, NB - 1:NBP, :], 0.0).then_inc(s_set, 1)
                    e.wait_ge(s_in, 48)
                    then_wait(e.tensor_reduce(mean[:, :], xs[:, :, :], AX, ALU.add))
                    then_wait(e.tensor_scalar(mean[:, :], mean[:, :], 1.0 / P, None, ALU.mult))
                    e.wait_ge(s_out, 16)
                    then_wait(e.tensor_tensor(xs[:, :, :], xs[:, :, :],
                                              mean[:, :].unsqueeze(2).broadcast_to([P, NBP, P]), ALU.subtract))
                    for q in range(0, NBP, G):
                        then_wait(e.tensor_tensor(sq[:, :, :], xs[:, q:q + G, :], xs[:, q:q + G, :], ALU.mult))
                        then_wait(e.tensor_reduce(var[:, q:q + G], sq[:, :, :], AX, ALU.add))
                    e.tensor_scalar(var[:, :], var[:, :], 1.0 / P, EPS, ALU.mult, ALU.add).then_inc(s_var, 1)
                    e.wait_ge(s_std, 1)
                    then_wait(e.reciprocal(rstd[:, :], std[:, :]))
                    for n, q in enumerate(range(0, NBP, G)):
                        wait(e, s_tr, n)
                        e.tensor_tensor(hn[:, :, :], xs[:, q:q + G, :], over_width(rstd[:, q:q + G], P), ALU.mult)\
                         .then_inc(s_hn, 1)
                        if n:
                            split(e, n - 1)
                    split(e, NBP // G - 1)

                @block.scalar
                def _(e):
                    e.wait_ge(s_var, 1)
                    e.activation(std[:, :], var[:, :], ACT.Sqrt).then_inc(s_std, 1)
                    for n in range(NBP // G):
                        e.wait_ge(s_tr, n + 1)
                        wait(e, s_hf, n)
                        e.activation(hT[:, :, :], ps_tr[:, :, :], ACT.Relu).then_inc(s_hT, 1)

                @block.tensor
                def _(e):
                    e.wait_ge(s_in, 48)
                    for n in range(NBP // G):
                        e.wait_ge(s_hn, n + 1)
                        wait(e, s_hT, n)
                        for k in range(G):
                            mm = e.transpose(ps_tr[:, k, :], hn[:, k, :], identf[:, :])
                        mm.then_inc(s_tr, 1)
                        e.wait_ge(s_hT, n + 1)
                        wait(e, s_sub, n)
                        for k in range(G):
                            mm = e.matmul(ps_hf[:, k, :], hT[:, k, :], win[:, :], start=True, stop=True)
                        mm.then_inc(s_hf, 1)

        with messages, ExitStack() as c:
            rec = [sb(f"rec{h}", [P, G, REC], c=c) for h in range(2)]
            skey = [sb(f"skey{h}", [P, G], c=c) for h in range(2)]
            here = [sb(f"here{h}", [P, G], c=c) for h in range(2)]
            kind = [sb(f"kind{h}", [P, G], c=c) for h in range(2)]
            hot = [sb(f"hot{h}", [P, G, NB], BF16, c) for h in range(2)]
            node = [sb(f"node{h}", [P, G, P], BF16, c) for h in range(2)]
            nodeT = [sb(f"nodeT{h}", [P, G, P], BF16, c) for h in range(2)]
            hott = [sb(f"hott{h}", [P, G, R], BF16, c) for h in range(2)]
            rank = sb("rank", [P, G, NB], c=c)
            posf = sb("posf", [P, G], c=c)
            pos = [sb(f"pos{h}", [P, G], I32, c) for h in range(2)]
            fT = [sb(f"fT{h}", [NRBF + 1, G * P], c=c) for h in range(2)]
            soft = [sb(f"soft{h}", [P, G * P], c=c) for h in range(2)]
            filt = [sb(f"filt{h}", [P, G, P], c=c) for h in range(2)]
            hcut = [sb(f"hcut{h}", [P, G, P], c=c) for h in range(2)]
            wij = sb("wij", [P, G, P], c=c)
            msg = [sb(f"msg{h}", [P, G, MSG], c=c) for h in range(2)]
            wf1 = sb("wf1", [NRBF + 1, P], c=c)
            wf2 = sb("wf2", [P, P], c=c)
            bf2 = sb("bf2", [P, P], c=c)
            half = sb("half", [P, 1], c=c)
            ranks = psum("ranks", [P, G, NB], c=c)
            ps_f = psum("ps_f", [P, G * P], c=c)
            ps_v = psum("ps_v", [P, G * P], c=c)
            ps_w = psum("ps_w", [P, G, P], c=c)
            ps_g = psum("ps_g", [P, G, P], c=c)
            ps_n = psum("ps_n", [P, G, P], BF16, c)
            ps_c = psum("ps_c", [P, G, R], c=c)
            s_w, s_set = sem("weights_loaded", c), sem("constants_set", c)
            s_rec = [sem(f"records_loaded{h}", c) for h in range(2)]
            s_msg = [sem(f"messages_stored{h}", c) for h in range(2)]
            s_loc, s_typ, s_key = sem("local_dst", c), sem("types", c), sem("src_keys", c)
            s_hot, s_node, s_hott = sem("hot_built", c), sem("node_hot_built", c), sem("type_hot_built", c)
            s_before, s_read, s_red = sem("ranks_ready", c), sem("ranks_read", c), sem("ranks_summed", c)
            s_pos, s_after = sem("positions_ready", c), sem("ranks_moved", c)
            s_fp, s_fT, s_vp = sem("basis_turned", c), sem("basis_copied", c), sem("filter1_product", c)
            s_abs, s_exp, s_log, s_filt = sem("abs", c), sem("exp", c), sem("log", c), sem("softplus_ready", c)
            s_np, s_nT, s_g, s_hc = sem("node_hot_turned", c), sem("node_hotT_copied", c), sem("hf_gathered", c), sem("hf_scaled", c)
            s_c, s_cadd = sem("type_counts", c), sem("counts_added", c)
            s_wp, s_wij, s_m, s_row = sem("filter2_product", c), sem("filter2_ready", c), sem("messages_ready", c), sem("row_tables", c)
            s_src = sem("message_src", c)
            with nc.Block() as block:

                @block.sync
                def _(e):
                    e.dma_start(wf1[0:NRBF, :], w_f1).then_inc(s_w, 16)
                    e.dma_start(wf1[NRBF:NRBF + 1, :], b_f1.rearrange("(a f) -> a f", a=1)).then_inc(s_w, 16)
                    e.dma_start(wf2[:, :], w_f2).then_inc(s_w, 16)
                    e.dma_start(bf2[:, :], b_f2.rearrange("(a f) -> a f", a=1).broadcast_to([P, P])).then_inc(s_w, 16)

                    def group(i, h):
                        g = 2 * i + h
                        wait(e, s_src, g - 1)
                        wait(e, s_pos, g - 1)
                        first = tile_values(e, 32, g * G, E)
                        for k in range(G):
                            e.dma_start(rec[h][:, k, :], recs[bass.ds(first[k], P), :]).then_inc(s_rec[h], 16)

                    halves(e, HALF_T, group)

                @block.vector
                def _(e):
                    def first_half(i, h):
                        g = 2 * i + h
                        tiles = bass.ds(g * G, G)
                        e.wait_ge(s_rec[h], (16 * G) * (i + 1))
                        e.tensor_tensor(here[h][:, :], rec[h][:, :, DST], blk_d[:, tiles], ALU.subtract).then_inc(s_loc, 1)
                        e.scalar_tensor_tensor(out=kind[h][:, :], in0=rec[h][:, :, SRC], scalar=-float(R),
                                               in1=rec[h][:, :, ROW], op0=ALU.mult, op1=ALU.add).then_inc(s_typ, 1)
                        e.wait_ge(s_loc, g + 1)
                        e.scalar_tensor_tensor(out=skey[h][:, :], in0=here[h][:, :], scalar=float(P),
                                               in1=rec[h][:, :, SBLK], op0=ALU.is_lt, op1=ALU.mult).then_inc(s_key, 1)
                        wait(e, s_after, g - 1)
                        e.tensor_tensor(node[h][:, :, :], over_groups(iota[:, 0:P], P), over_width(here[h][:, :], P),
                                        ALU.is_equal).then_inc(s_node, 1)
                        e.wait_ge(s_key, g + 1)
                        e.tensor_tensor(hot[h][:, :, :], over_groups(iota[:, 1:NB + 1], NB), over_width(skey[h][:, :], NB),
                                        ALU.is_equal).then_inc(s_hot, 1)
                        e.wait_ge(s_typ, g + 1)
                        e.tensor_tensor(hott[h][:, :, :], over_groups(iota[:, 0:R], R), over_width(kind[h][:, :], R),
                                        ALU.is_equal).then_inc(s_hott, 1)
                        wait(e, s_red, g)
                        e.wait_ge(s_before, g + 1)
                        e.tensor_tensor(rank[:, :, :], ranks[:, :, :], hot[h][:, :, :], ALU.mult).then_inc(s_read, 1)
                        e.wait_ge(s_read, g + 1)
                        e.tensor_reduce(posf[:, :], rank[:, :, :], AX, ALU.add).then_inc(s_red, 1)
                        e.wait_ge(s_red, g + 1)
                        wait(e, s_msg[h], i * (16 * G))
                        e.tensor_scalar(pos[h][:, :], posf[:, :], AHEAD, None, ALU.add).then_inc(s_pos, 1)
                        e.wait_ge(s_c, g + 1)
                        block16 = tile_values(e, 0, g * G, R * (NB - 1))
                        for k in range(G):
                            wait(e, s_cadd, g * G + k)
                            at = counts[:, bass.ds(block16[k], R)]
                            e.tensor_tensor(at, at, ps_c[:, k, :], ALU.add).then_inc(s_cadd, 1)
                        e.wait_ge(s_log, g + 1)
                        e.scalar_tensor_tensor(out=filt[h][:, :, :], in0=ps_v[:, :].rearrange("p (k n) -> p k n", k=G),
                                               scalar=0.0, in1=soft[h][:, :].rearrange("p (k n) -> p k n", k=G),
                                               op0=ALU.max, op1=ALU.add).then_inc(s_filt, 1)

                    def second_half(i, h):
                        g = 2 * i + h
                        e.wait_ge(s_wp, g + 1)
                        wait(e, s_m, g)
                        e.tensor_tensor(wij[:, :, :], ps_w[:, :, :], over_groups(bf2[:, :], P), ALU.add).then_inc(s_wij, 1)
                        e.wait_ge(s_wij, g + 1)
                        e.wait_ge(s_hc, g + 1)
                        wait(e, s_msg[h], i * (16 * G))
                        e.tensor_tensor(msg[h][:, :, 0:P], wij[:, :, :], hcut[h][:, :, :], ALU.mult).then_inc(s_m, 1)

                    e.memset(counts[:, :], 0.0).then_inc(s_set, 1)
                    e.memset(half[:, :], 0.5).then_inc(s_set, 1)
                    for h in range(2):
                        ins = e.memset(fT[h][:, :], 1.0)
                    ins.then_inc(s_set, 1)
                    e.wait_ge(s_w, 64)
                    e.wait_ge(s_set, 3)
                    staggered(e, HALF_T, first_half, second_half)

                @block.scalar
                def _(e):
                    def first_half(i, h):
                        g = 2 * i + h
                        tiles = bass.ds(g * G, G)
                        e.wait_ge(s_loc, g + 1)
                        settle(e)
                        e.activation(loc[:, tiles], here[h][:, :], ACT.Copy)
                        e.activation(row[:, tiles], rec[h][:, :, ROW], ACT.Copy).then_inc(s_row, 1)
                        e.wait_ge(s_typ, g + 1)
                        settle(e)
                        e.activation(typ[:, tiles], kind[h][:, :], ACT.Copy)
                        e.wait_ge(s_fp, g + 1)
                        e.activation(fT[h][0:NRBF, :], ps_f[0:NRBF, :], ACT.Copy).then_inc(s_fT, 1)
                        e.wait_ge(s_np, g + 1)
                        e.activation(nodeT[h][:, :, :], ps_n[:, :, :], ACT.Copy).then_inc(s_nT, 1)
                        e.wait_ge(s_vp, g + 1)
                        e.activation(soft[h][:, :], ps_v[:, :], ACT.Abs).then_inc(s_abs, 1)
                        e.wait_ge(s_abs, g + 1)
                        e.activation(soft[h][:, :], soft[h][:, :], ACT.Exp, scale=-1.0).then_inc(s_exp, 1)
                        e.wait_ge(s_exp, g + 1)
                        e.activation(soft[h][:, :], soft[h][:, :], ACT.Ln, scale=0.5, bias=half[:, 0:1]).then_inc(s_log, 1)
                        e.wait_ge(s_g, g + 1)
                        wait(e, s_m, g - 1)
                        for k in range(G):
                            ins = e.activation(hcut[h][:, k, :], ps_g[:, k, :], ACT.Copy, scale=rec[h][:, k, CUT:CUT + 1])
                        ins.then_inc(s_hc, 1)
                        wait(e, s_msg[h], i * (16 * G))
                        e.activation(msg[h][:, :, P:MSG], rec[h][:, :, SRC:SRC + 1], ACT.Copy).then_inc(s_src, 1)

                    e.wait_ge(s_set, 3)
                    halves(e, HALF_T, first_half)

                @block.tensor
                def _(e):
                    def first_half(i, h):
                        g = 2 * i + h
                        e.wait_ge(s_rec[h], (16 * G) * (i + 1))
                        wait(e, s_fT, g)
                        for k in range(G):
                            mm = e.transpose(ps_f[0:NRBF, k * P:(k + 1) * P], rec[h][:, k, 0:NRBF], identf[:, :])
                        mm.then_inc(s_fp, 1)
                        e.wait_ge(s_node, g + 1)
                        wait(e, s_nT, g)
                        for k in range(G):
                            mm = e.transpose(ps_n[:, k, :], node[h][:, k, :], identb[:, :])
                        mm.then_inc(s_np, 1)
                        e.wait_ge(s_fT, g + 1)
                        wait(e, s_filt, g)
                        e.matmul(ps_v[:, :], wf1[:, :], fT[h][:, :], start=True, stop=True).then_inc(s_vp, 1)
                        e.wait_ge(s_hot, g + 1)
                        rank_before(e, ranks, hot[h]).then_inc(s_before, 1)
                        e.wait_ge(s_nT, g + 1)
                        wait(e, s_hc, g)
                        block16 = tile_values(e, 0, g * G, R * (NB - 1))
                        for k in range(G):
                            for part in range(3):
                                mm = e.matmul(ps_g[:, k, :], nodeT[h][:, k, :],
                                              hf_rows[:, bass.ds(block16[k] * (3 * P // R) + part * P, P)],
                                              start=(part == 0), stop=(part == 2))
                        mm.then_inc(s_g, 1)
                        e.wait_ge(s_hott, g + 1)
                        wait(e, s_cadd, g * G)
                        for k in range(G):
                            mm = e.matmul(ps_c[:, k, :], node[h][:, k, :], hott[h][:, k, :], start=True, stop=True)
                        mm.then_inc(s_c, 1)
                        e.wait_ge(s_read, g + 1)
                        rank_after(e, ranks, hot[h]).then_inc(s_after, 1)

                    def second_half(i, h):
                        g = 2 * i + h
                        e.wait_ge(s_filt, g + 1)
                        wait(e, s_wij, g)
                        for k in range(G):
                            mm = e.matmul(ps_w[:, k, :], filt[h][:, k, :], wf2[:, :], start=True, stop=True)
                        mm.then_inc(s_wp, 1)

                    hf_rows = hf[:, :, :, :].rearrange("p b t f -> p (b t f)")
                    e.wait_ge(s_w, 64)
                    rank_start(e, ranks, 1)
                    staggered(e, HALF_T, first_half, second_half)

                @block.gpsimd
                def _(e):
                    def group(i, h):
                        g = 2 * i + h
                        e.wait_ge(s_m, g + 1)
                        e.wait_ge(s_src, g + 1)
                        e.wait_ge(s_pos, g + 1)
                        settle(e)
                        for k in range(G):
                            e.indirect_dma_start(
                                out=msgs, out_offset=bass.IndirectOffsetOnAxis(ap=pos[h][:, k:k + 1], axis=0),
                                in_=msg[h][:, k, :], in_offset=None, bounds_check=E - 1, oob_is_err=False)\
                             .then_inc(s_msg[h], 16)

                    halves(e, HALF_T, group)
                    for h in range(2):
                        e.wait_ge(s_msg[h], HALF_T * 16 * G)

        acc = sb("acc", [P, NBP * P])

        def add_tiles(e, g, block16, sums, s_add):
            for k in range(G):
                wait(e, s_add, g * G + k)
                at = acc[:, bass.ds(block16[k] * (P // R), P)]
                e.tensor_tensor(at, at, sums[:, k, :], ALU.add).then_inc(s_add, 1)

        with ExitStack() as c:
            inv = sb("inv", [P, NB * R], c=c)
            inv3 = sb("inv3", [P, NB, 3, R], BF16, c)
            msg = [sb(f"msg{h}", [P, G, MSG], c=c) for h in range(2)]
            here = [sb(f"here{h}", [P, G], c=c) for h in range(2)]
            nodes = [sb(f"nodes{h}", [P, G, P], c=c) for h in range(2)]
            node = [sb(f"node{h}", [P, G, P], BF16, c) for h in range(2)]
            nodeT = [sb(f"nodeT{h}", [P, G, P], BF16, c) for h in range(2)]
            hott = [sb(f"hott{h}", [P, G, R], BF16, c) for h in range(2)]
            pick = sb("pick", [P, G, 3, R], c=c)
            ps_a = [psum(f"ps_a{h}", [P, G, P], c=c) for h in range(2)]
            ps_n = [psum(f"ps_n{h}", [P, G, P], BF16, c) for h in range(2)]
            ps_i = [psum(f"ps_i{h}", [P, G, 3, R], c=c) for h in range(2)]
            s_msg = [sem(f"messages_loaded{h}", c) for h in range(2)]
            s_v, s_inv, s_acc = sem("dve_step", c), sem("inverse_ready", c), sem("sums_cleared", c)
            s_here, s_nodes, s_node, s_hott = sem("local_src", c), sem("src_hot", c), sem("dst_hot", c), sem("type_hot", c)
            s_prod, s_add = sem("sums_ready", c), sem("sums_added", c)
            s_np, s_nT, s_ip, s_pick, s_w = (sem("dst_hot_turned", c), sem("dst_hotT_copied", c), sem("inverse_rows", c),
                                             sem("inverse_picked", c), sem("weights_ready", c))
            with nc.Block() as block:

                @block.sync
                def _(e):
                    def group(i, h):
                        g = 2 * i + h
                        wait(e, s_prod, g - 1)
                        first = tile_values(e, 96, g * G, E)
                        for k in range(G):
                            e.dma_start(msg[h][:, k, :], msgs[bass.ds(first[k], P), :]).then_inc(s_msg[h], 16)

                    halves(e, HALF_T, group)

                @block.vector
                def _(e):
                    steps = [0]

                    def then_wait(ins):
                        steps[0] += 1
                        ins.then_inc(s_v, 1)
                        e.wait_ge(s_v, steps[0])

                    def first_half(i, h):
                        g = 2 * i + h
                        tiles = bass.ds(g * G, G)
                        wait(e, s_ip, g - 1)
                        wait(e, s_prod, g - 1)
                        e.tensor_tensor(node[h][:, :, :], over_groups(iota[:, 0:P], P), over_width(loc[:, tiles], P),
                                        ALU.is_equal).then_inc(s_node, 1)
                        e.wait_ge(s_msg[h], (16 * G) * (i + 1))
                        e.tensor_tensor(here[h][:, :], msg[h][:, :, P], blk_s[:, tiles], ALU.subtract).then_inc(s_here, 1)
                        e.tensor_tensor(hott[h][:, :, :], over_groups(iota[:, 0:R], R), over_width(typ[:, tiles], R),
                                        ALU.is_equal).then_inc(s_hott, 1)
                        e.wait_ge(s_here, g + 1)
                        e.tensor_tensor(nodes[h][:, :, :], over_groups(iota[:, 0:P], P), over_width(here[h][:, :], P),
                                        ALU.is_equal).then_inc(s_nodes, 1)

                    def second_half(i, h):
                        g = 2 * i + h
                        e.wait_ge(s_ip, g + 1)
                        wait(e, s_w, g)
                        e.wait_ge(s_hott, g + 1)
                        e.tensor_tensor(pick[:, :, :, :], ps_i[h][:, :, :, :],
                                        hott[h][:, :, :].unsqueeze(2).broadcast_to([P, G, 3, R]), ALU.mult).then_inc(s_pick, 1)
                        e.wait_ge(s_prod, g + 1)
                        block16 = tile_values(e, 64, g * G, R * (NB - 1))
                        add_tiles(e, g, block16, ps_a[h], s_add)
                        e.wait_ge(s_pick, g + 1)
                        settle(e)
                        e.tensor_reduce(wgt[:, bass.ds(g * G, G)], pick[:, :, :, :].rearrange("p k t r -> p k (t r)"),
                                        AX, ALU.add).then_inc(s_w, 1)

                    e.memset(acc[:, :], 0.0).then_inc(s_acc, 1)
                    then_wait(e.tensor_scalar(inv[:, :], counts[:, :], 1.0, None, ALU.max))
                    then_wait(e.reciprocal(inv[:, :], inv[:, :]))
                    blocks = inv[:, :].rearrange("p (b r) -> p b r", r=R)
                    then_wait(e.tensor_copy(inv3[:, :, 0, :], blocks))
                    then_wait(e.tensor_tensor(blocks, blocks, inv3[:, :, 0, :], ALU.subtract))
                    then_wait(e.tensor_copy(inv3[:, :, 1, :], blocks))
                    e.tensor_tensor(inv3[:, :, 2, :], blocks, inv3[:, :, 1, :], ALU.subtract).then_inc(s_inv, 1)
                    e.wait_ge(s_acc, 1)
                    staggered(e, HALF_T, first_half, second_half)

                @block.scalar
                def _(e):
                    def group(i, h):
                        g = 2 * i + h
                        e.wait_ge(s_np, g + 1)
                        wait(e, s_ip, g - 1)
                        e.activation(nodeT[h][:, :, :], ps_n[h][:, :, :], ACT.Copy).then_inc(s_nT, 1)

                    halves(e, HALF_T, group)

                @block.tensor
                def _(e):
                    def first_half(i, h):
                        g = 2 * i + h
                        e.wait_ge(s_node, g + 1)
                        wait(e, s_nT, g - 1)
                        for k in range(G):
                            mm = e.transpose(ps_n[h][:, k, :], node[h][:, k, :], identb[:, :])
                        mm.then_inc(s_np, 1)
                        e.wait_ge(s_nodes, g + 1)
                        wait(e, s_add, (g - 1) * G)
                        for k in range(G):
                            mm = e.matmul(ps_a[h][:, k, :], msg[h][:, k, 0:P], nodes[h][:, k, :], start=True, stop=True)
                        mm.then_inc(s_prod, 1)

                    def second_half(i, h):
                        g = 2 * i + h
                        e.wait_ge(s_nT, g + 1)
                        wait(e, s_pick, g - 1)
                        block16 = tile_values(e, 0, g * G, R * (NB - 1))
                        for k in range(G):
                            mm = e.matmul(ps_i[h][:, k, :, :].rearrange("p t r -> p (t r)"), nodeT[h][:, k, :],
                                          inv_rows[:, bass.ds(block16[k] * 3, 3 * R)], start=True, stop=True)
                        mm.then_inc(s_ip, 1)

                    inv_rows = inv3[:, :, :, :].rearrange("p b t r -> p (b t r)")
                    e.wait_ge(s_inv, 1)
                    staggered(e, HALF_T, first_half, second_half)

        normed = ExitStack()
        hx = sb("hx", [P, NBP, P], c=normed)
        rstd = sb("rstd", [P, NBP], c=normed)
        with ExitStack() as c:
            NW = G * P
            wo1 = sb("wo1", [P, P], c=c)
            wo2 = sb("wo2", [P, P], c=c)
            bo1 = sb("bo1", [P, 1], c=c)
            bo2 = sb("bo2", [P, P], c=c)
            half = sb("half", [P, 1], c=c)
            var = sb("var", [P, NBP], c=c)
            soft = sb("soft", [P, NW], c=c)
            act = sb("act", [P, NW], c=c)
            xl = [sb(f"xl{h}", [P, G, P], c=c) for h in range(2)]
            x1 = [sb(f"x1_{h}", [P, G, P], c=c) for h in range(2)]
            tot = sb("tot", [P, G], c=c)
            sq = sb("sq", [P, G, P], c=c)
            ps_v = psum("ps_v", [P, NW], c=c)
            ps_o = psum("ps_o", [P, G, P], c=c)
            s_w, s_half = sem("weights_loaded", c), sem("half_set", c)
            s_x = [sem(f"x_loaded{h}", c) for h in range(2)]
            s_st = [sem(f"x1_stored{h}", c) for h in range(2)]
            s_vp, s_abs, s_exp, s_log, s_pos = sem("product1", c), sem("abs", c), sem("exp", c), sem("log", c), sem("positive", c)
            s_act, s_op, s_v, s_x1, s_c = sem("softplus_ready", c), sem("product2", c), sem("dve_step", c), sem("x1_ready", c), sem("centered", c)
            s_sq, s_var, s_std = sem("squared", c), sem("variances_ready", c), sem("std_ready", c)
            with nc.Block() as block:
                NGR = NBP // G

                def normalise(e, n):
                    h = n % 2
                    rows = slice(n * G, (n + 1) * G)
                    e.wait_ge(s_op, n + 1)
                    e.wait_ge(s_x[h], 16 * (n // 2 + 1))
                    wait(e, s_st[h], 16 * (n // 2))
                    e.tensor_tensor(x1[h][:, :, :], ps_o[:, :, :], over_groups(bo2[:, :], P), ALU.add).then_inc(s_v, 1)
                    e.wait_ge(s_v, n + 1)
                    e.tensor_tensor(x1[h][:, :, :], x1[h][:, :, :], xl[h][:, :, :], ALU.add).then_inc(s_x1, 1)
                    e.wait_ge(s_x1, n + 1)
                    e.tensor_reduce(tot[:, :], x1[h][:, :, :], AX, ALU.add).then_inc(s_c, 1)
                    e.wait_ge(s_c, 3 * n + 1)
                    e.tensor_scalar(tot[:, :], tot[:, :], 1.0 / P, None, ALU.mult).then_inc(s_c, 1)
                    e.wait_ge(s_c, 3 * n + 2)
                    e.tensor_tensor(hx[:, rows, :], x1[h][:, :, :], over_width(tot[:, :], P), ALU.subtract).then_inc(s_c, 1)
                    e.wait_ge(s_c, 3 * n + 3)
                    e.tensor_tensor(sq[:, :, :], hx[:, rows, :], hx[:, rows, :], ALU.mult).then_inc(s_sq, 1)
                    e.wait_ge(s_sq, 2 * n + 1)
                    e.tensor_reduce(var[:, rows], sq[:, :, :], AX, ALU.add).then_inc(s_sq, 1)
                    e.wait_ge(s_sq, 2 * n + 2)

                def store(e, n):
                    h = n % 2
                    e.wait_ge(s_x1, n + 1)
                    e.dma_start(x1d[n * NW:(n + 1) * NW, :].rearrange("(k p) f -> p k f", p=P), x1[h][:, :, :])\
                     .then_inc(s_st[h], 16)

                @block.sync
                def _(e):
                    e.dma_start(wo1[:, :], w_o1).then_inc(s_w, 16)
                    e.dma_start(wo2[:, :], w_o2).then_inc(s_w, 16)
                    e.dma_start(bo1[:, :], b_o1.rearrange("(f a) -> f a", a=1)).then_inc(s_w, 16)
                    e.dma_start(bo2[:, :], b_o2.rearrange("(a f) -> a f", a=1).broadcast_to([P, P])).then_inc(s_w, 16)
                    for n in range(NGR):
                        h = n % 2
                        rows = slice(n * NW, (n + 1) * NW)
                        wait(e, s_x1, n - 1)
                        e.dma_start(xl[h][:, :, :], xpad[rows, :].rearrange("(k p) f -> p k f", p=P)).then_inc(s_x[h], 16)
                        if n:
                            store(e, n - 1)
                    store(e, NGR - 1)
                    for h in range(2):
                        e.wait_ge(s_st[h], 16 * ((NGR - h + 1) // 2))

                @block.scalar
                def _(e):
                    e.wait_ge(s_w, 64)
                    e.wait_ge(s_half, 1)
                    for n in range(NGR):
                        e.wait_ge(s_vp, n + 1)
                        wait(e, s_act, n)
                        e.activation(soft[:, :], ps_v[:, :], ACT.Abs, bias=bo1[:, 0:1]).then_inc(s_abs, 1)
                        e.wait_ge(s_abs, n + 1)
                        e.activation(soft[:, :], soft[:, :], ACT.Exp, scale=-1.0).then_inc(s_exp, 1)
                        e.wait_ge(s_exp, n + 1)
                        e.activation(soft[:, :], soft[:, :], ACT.Ln, scale=0.5, bias=half[:, 0:1]).then_inc(s_log, 1)
                    e.wait_ge(s_var, 1)
                    e.activation(var[:, :], var[:, :], ACT.Sqrt).then_inc(s_std, 1)

                @block.tensor
                def _(e):
                    e.wait_ge(s_w, 64)
                    for n in range(NGR + 1):
                        if n < NGR:
                            wait(e, s_pos, n)
                            wait(e, s_abs, n)
                            e.matmul(ps_v[:, :], wo1[:, :], acc[:, n * NW:(n + 1) * NW], start=True, stop=True)\
                             .then_inc(s_vp, 1)
                        if n:
                            e.wait_ge(s_act, n)
                            wait(e, s_v, n - 1)
                            for k in range(G):
                                mm = e.matmul(ps_o[:, k, :], act[:, k * P:(k + 1) * P], wo2[:, :], start=True, stop=True)
                            mm.then_inc(s_op, 1)

                @block.vector
                def _(e):
                    e.memset(half[:, :], 0.5).then_inc(s_half, 1)
                    e.wait_ge(s_w, 64)
                    e.wait_ge(s_half, 1)
                    for n in range(NGR + 1):
                        if n < NGR:
                            e.wait_ge(s_vp, n + 1)
                            e.wait_ge(s_abs, n + 1)
                            wait(e, s_op, n)
                            e.tensor_scalar(act[:, :], ps_v[:, :], bo1[:, 0:1], 0.0, ALU.add, ALU.max).then_inc(s_pos, 1)
                            e.wait_ge(s_pos, n + 1)
                            e.wait_ge(s_log, n + 1)
                            e.tensor_tensor(act[:, :], act[:, :], soft[:, :], ALU.add).then_inc(s_act, 1)
                        if n:
                            normalise(e, n - 1)
                    e.wait_ge(s_sq, 2 * NGR)
                    e.tensor_scalar(var[:, :], var[:, :], 1.0 / P, EPS, ALU.mult, ALU.add).then_inc(s_var, 1)
                    e.wait_ge(s_std, 1)
                    e.reciprocal(rstd[:, :], var[:, :])

        s_w, s_st = sem("layer_weights_loaded"), [sem(f"products_stored{h}") for h in range(2)]
        s_hn, s_tr, s_hT, s_rp, s_root = (sem("h_ready"), sem("h_turned"), sem("hT_ready"),
                                          sem("root_product"), sem("root_added"))
        s_yp, s_yv, s_ya = sem("products_ready"), sem("products_copied_dve"), sem("products_copied_act")
        s_idx, s_hot, s_prod, s_add = sem("indices_ready"), sem("weighted_hot"), sem("sums_ready"), sem("sums_added")
        for layer in range(LAYERS):
            B0, T0 = layer * (NB // 2), layer * HALF_T
            with (normed if layer == 0 else ExitStack()), ExitStack() as c:
                wl = sb("wl", [P, R * P], c=c)
                wr = sb("wr", [P, P], c=c)
                bl = sb("bl", [P, 1], c=c)
                hn = [sb(f"hn{h}", [P, P], c=c) for h in range(2)]
                hT = [sb(f"hT{h}", [P, P], c=c) for h in range(2)]
                yst = [sb(f"yst{h}", [P, R * P], c=c) for h in range(2)]
                ps_t = [psum(f"ps_t{h}", [P, P], c=c) for h in range(2)]
                ps_r = [psum(f"ps_r{h}", [P, P], c=c) for h in range(2)]
                ps_y = [psum(f"ps_y{q}", [P, 512], c=c) for q in range(4)]
                with nc.Block() as block:

                    @block.sync
                    def _(e):
                        e.dma_start(wl[:, :].rearrange("i (r o) -> i r o", r=R), w_rel[layer].rearrange("r i o -> i r o"))\
                         .then_inc(s_w, 16)
                        e.dma_start(wr[:, :], w_root[layer]).then_inc(s_w, 16)
                        e.dma_start(bl[:, :], bias_rel[layer].rearrange("(f a) -> f a", a=1)).then_inc(s_w, 16)

                        def group(i, h):
                            m = 2 * i + h
                            n = 2 * (B0 + i) + h
                            e.wait_ge(s_yv, 2 * (n + 1))
                            e.wait_ge(s_ya, 2 * (n + 1))
                            e.dma_start(ytab[bass.ds(m * P, P), :], yst[h][:, :]).then_inc(s_st[h], 16)

                        halves(e, NB // 2, group)
                        for h in range(2):
                            e.wait_ge(s_st[h], 16 * (B0 + NB // 2))

                    @block.vector
                    def _(e):
                        def first_half(i, h):
                            m = 2 * i + h
                            n = 2 * (B0 + i) + h
                            if layer == 0:
                                wait(e, s_tr, m - 1)
                                e.tensor_scalar(hn[h][:, :], hx_rows[:, bass.ds(m * P, P)], rstd[:, bass.ds(m, 1)], None,
                                                ALU.mult).then_inc(s_hn, 1)

                        def second_half(i, h):
                            m = 2 * i + h
                            n = 2 * (B0 + i) + h
                            wait(e, s_st[h], 16 * (B0 + i))
                            for q in (0, 2):
                                e.wait_ge(s_yp, 4 * n + q + 1)
                                e.tensor_copy(yst[h][:, q * 512:(q + 1) * 512], ps_y[q][:, :]).then_inc(s_yv, 1)

                        hx_rows = hx[:, :, :].rearrange("p m f -> p (m f)")
                        staggered(e, NB // 2, first_half, second_half)

                    @block.scalar
                    def _(e):
                        def first_half(i, h):
                            m = 2 * i + h
                            n = 2 * (B0 + i) + h
                            wait(e, s_yp, 4 * (n - 1))
                            if layer == 0:
                                e.wait_ge(s_tr, m + 1)
                                e.activation(hT[h][:, :], ps_t[h][:, :], ACT.Relu).then_inc(s_hT, 1)
                            else:
                                settle(e)
                                e.activation(hT[h][:, :], acc[:, bass.ds(m * P, P)], ACT.Relu).then_inc(s_hT, 1)

                        def second_half(i, h):
                            m = 2 * i + h
                            n = 2 * (B0 + i) + h
                            e.wait_ge(s_rp, n + 1)
                            e.wait_ge(s_hT, n + 1)
                            settle(e)
                            e.activation(acc[:, bass.ds(m * P, P)], ps_r[h][:, :], ACT.Identity, bias=bl[:, 0:1])\
                             .then_inc(s_root, 1)
                            wait(e, s_st[h], 16 * (B0 + i))
                            for q in (1, 3):
                                e.wait_ge(s_yp, 4 * n + q + 1)
                                e.activation(yst[h][:, q * 512:(q + 1) * 512], ps_y[q][:, :], ACT.Copy).then_inc(s_ya, 1)

                        e.wait_ge(s_w, 48 * (layer + 1))
                        staggered(e, NB // 2, first_half, second_half)

                    @block.tensor
                    def _(e):
                        def first_half(i, h):
                            m = 2 * i + h
                            n = 2 * (B0 + i) + h
                            if layer == 0:
                                e.wait_ge(s_hn, m + 1)
                                wait(e, s_hT, m - 1)
                                e.transpose(ps_t[h][:, :], hn[h][:, :], identf[:, :]).then_inc(s_tr, 1)

                        def second_half(i, h):
                            m = 2 * i + h
                            n = 2 * (B0 + i) + h
                            e.wait_ge(s_hT, n + 1)
                            wait(e, s_root, n - 1)
                            e.matmul(ps_r[h][:, :], wr[:, :], hT[h][:, :], start=True, stop=True).then_inc(s_rp, 1)
                            for q in range(4):
                                wait(e, (s_yv, s_ya)[q % 2], 2 * n - 1 + q // 2)
                                e.matmul(ps_y[q][:, :], hT[h][:, :], wl[:, q * 512:(q + 1) * 512], start=True, stop=True)\
                                 .then_inc(s_yp, 1)

                        e.wait_ge(s_w, 48 * (layer + 1))
                        staggered(e, NB // 2, first_half, second_half)

            with ExitStack() as c:
                idx = [sb(f"idx{h}", [P, G], I32, c) for h in range(2)]
                got = [sb(f"got{h}", [P, G, P], c=c) for h in range(2)]
                hotw = [sb(f"hotw{h}", [P, G, P], c=c) for h in range(2)]
                ps_a = [psum(f"ps_a{h}", [P, G, P], c=c) for h in range(2)]
                s_got = [sem(f"rows_gathered{h}", c) for h in range(2)]
                with nc.Block() as block:

                    @block.scalar
                    def _(e):
                        def group(i, h):
                            g = 2 * i + h
                            n = 2 * (T0 + i) + h
                            wait(e, s_got[h], (16 * G) * i)
                            settle(e)
                            e.activation(idx[h][:, :], row[:, bass.ds(g * G, G)], ACT.Copy).then_inc(s_idx, 1)

                        halves(e, HALF_T, group)

                    @block.gpsimd
                    def _(e):
                        def group(i, h):
                            g = 2 * i + h
                            n = 2 * (T0 + i) + h
                            e.wait_ge(s_idx, n + 1)
                            wait(e, s_prod, n - 1)
                            settle(e)
                            for k in range(G):
                                e.indirect_dma_start(
                                    out=got[h][:, k, :], out_offset=None, in_=yrows,
                                    in_offset=bass.IndirectOffsetOnAxis(ap=idx[h][:, k:k + 1], axis=0),
                                    bounds_check=NB * P * R - 1, oob_is_err=False).then_inc(s_got[h], 16)

                        halves(e, HALF_T, group)

                    @block.vector
                    def _(e):
                        def first_half(i, h):
                            g = 2 * i + h
                            n = 2 * (T0 + i) + h
                            wait(e, s_prod, n - 1)
                            for k in range(G):
                                tile = bass.ds(g * G + k, 1)
                                ins = e.tensor_scalar(hotw[h][:, k, :], iota[:, 0:P], loc[:, tile], wgt[:, tile],
                                                      ALU.is_equal, ALU.mult)
                            ins.then_inc(s_hot, 1)

                        def second_half(i, h):
                            g = 2 * i + h
                            n = 2 * (T0 + i) + h
                            e.wait_ge(s_prod, n + 1)
                            block16 = tile_values(e, 0, g * G, R * (NB - 1))
                            add_tiles(e, n, block16, ps_a[h], s_add)

                        staggered(e, HALF_T, first_half, second_half)

                    @block.tensor
                    def _(e):
                        def group(i, h):
                            g = 2 * i + h
                            n = 2 * (T0 + i) + h
                            e.wait_ge(s_hot, n + 1)
                            e.wait_ge(s_got[h], (16 * G) * (i + 1))
                            wait(e, s_add, (n - 1) * G)
                            for k in range(G):
                                mm = e.matmul(ps_a[h][:, k, :], got[h][:, k, :], hotw[h][:, k, :], start=True, stop=True)
                            mm.then_inc(s_prod, 1)

                        halves(e, HALF_T, group)

        with ExitStack() as c:
            x1 = [sb(f"x1_{h}", [P, G, P], c=c) for h in range(2)]
            res = [sb(f"res{h}", [P, G, P], c=c) for h in range(2)]
            ps_t = [psum(f"ps_t{h}", [P, G, P], c=c) for h in range(2)]
            s_x = [sem(f"x1_loaded{h}", c) for h in range(2)]
            s_out = [sem(f"out_stored{h}", c) for h in range(2)]
            s_tr, s_res = sem("sums_turned", c), sem("result_ready", c)
            NGR = NBP // G
            with nc.Block() as block:

                @block.sync
                def _(e):
                    for n in range(NGR + 1):
                        h = n % 2
                        if n < NGR:
                            wait(e, s_res, n - 1)
                            e.dma_start(x1[h][:, :, :], x1d[n * G * P:(n + 1) * G * P, :].rearrange("(k p) f -> p k f", p=P))\
                             .then_inc(s_x[h], 16)
                        if n:
                            g, b = 1 - h, (n - 1) * G
                            e.wait_ge(s_res, n)
                            full = min(G, NB - 1 - b)
                            e.dma_start(out[b * P:(b + full) * P, :].rearrange("(k p) f -> p k f", p=P),
                                        res[g][:, 0:full, :]).then_inc(s_out[g], 16)
                            if full < G:
                                e.dma_start(out[(NB - 1) * P:N, :], res[g][0:LAST, full, :]).then_inc(s_out[g], 16)
                    for h in range(2):
                        extra = (NGR - 1) % 2 == h
                        e.wait_ge(s_out[h], 16 * ((NGR - h + 1) // 2 + extra))

                @block.vector
                def _(e):
                    for n in range(NGR):
                        h = n % 2
                        e.wait_ge(s_tr, n + 1)
                        e.wait_ge(s_x[h], 16 * (n // 2 + 1))
                        wait(e, s_out[h], 16 * (n // 2))
                        e.tensor_tensor(res[h][:, :, :], ps_t[h][:, :, :], x1[h][:, :, :], ALU.add).then_inc(s_res, 1)

                @block.tensor
                def _(e):
                    for n in range(NGR):
                        wait(e, s_res, n - 1)
                        for k in range(G):
                            b = n * G + k
                            mm = e.transpose(ps_t[n % 2][:, k, :], acc[:, b * P:(b + 1) * P], identf[:, :])
                        mm.then_inc(s_tr, 1)


_INS = ['x', 'src', 'dst', 'edge_attr_20', 'edge_type_16', 'edge_weight', 'L0_gnn_W_in2f', 'L0_gnn_W_filt1',
        'L0_gnn_b_filt1', 'L0_gnn_W_filt2', 'L0_gnn_b_filt2', 'L0_gnn_W_out1', 'L0_gnn_b_out1', 'L0_gnn_W_out2',
        'L0_gnn_b_out2', 'L1_gnn_W', 'L1_gnn_root', 'L1_gnn_bias']


def kernel(**inputs):
    import numpy as _np
    import concourse.bacc as _bacc
    from concourse import mybir as _mybir
    from concourse.bass_utils import run_bass_kernel_spmd as _run

    nc = _bacc.Bacc("TRN2", target_bir_lowering=False, num_devices=1)
    arrays, args = {}, []
    for name in _INS:
        a = _np.ascontiguousarray(inputs[name])
        arrays[f"in_{name}_dram"] = a
        args.append(nc.dram_tensor(f"in_{name}_dram", a.shape, _mybir.dt.from_np(a.dtype), kind="ExternalInput").ap())
    args.append(nc.dram_tensor("out_0_dram", inputs["x"].shape, _mybir.dt.float32, kind="ExternalOutput").ap())
    gnn_kernel(nc, *args)
    r = _run(nc, [arrays], core_ids=[0])
    return r.results[0]["out_0_dram"]
```

```python
from contextlib import ExitStack

import concourse.bass as bass
from concourse import mybir

P = 128
G = 4
R = 16
NRBF = 20
HIGH, MID, LOW = range(3)
STACK = [(HIGH, HIGH), (HIGH, MID), (HIGH, LOW), (MID, HIGH), (MID, MID), (LOW, HIGH)]
ONES = len(STACK) * NRBF
KF = ONES + 3
WORDS = (KF + 1) // 2
AUX = 5
REC = WORDS + AUX
CUT, DST, ROW, SBLK, SRC = range(WORDS, REC)
RG = 2
MSG = P + 1
AHEAD = float(1 << 18)
EPS = 1e-5

ALU = mybir.AluOpType
ACT = mybir.ActivationFunctionType
AX = mybir.AxisListType.X
F32 = mybir.dt.float32
BF16 = mybir.dt.bfloat16
I32 = mybir.dt.int32


def ceil_to(n, m):
    return (n + m - 1) // m * m


def gnn_kernel(nc, x, src, dst, edge_attr, edge_type, edge_weight, w_in, w_f1, b_f1, w_f2, b_f2,
               w_o1, b_o1, w_o2, b_o2, w_rel, w_root, bias_rel, out):
    N = x.shape[0]
    E = src.shape[0]
    LAYERS = w_rel.shape[0]
    NB = -(-N // P)
    NBP = ceil_to(NB, G)
    TE = ceil_to(-(-E // P), 2 * G)
    T = ceil_to((E + (P - 1) * NB) // P, 4 * G)
    NG = TE // G
    FULL = E // (G * P)
    REST = E - FULL * G * P
    CHUNKS = next(d for d in range(-(-NG // P), NG + 1) if NG % d == 0)
    CR = NG // CHUNKS
    HALF_E, HALF_T = TE // (2 * G), T // (2 * G)
    LAST = N - (NB - 1) * P
    WIDE = 4 if HALF_E % 4 == 0 and HALF_E // 4 > 3 else 1
    QUARTERS = R * P // 512
    NR = P // QUARTERS
    GROUPS = T // G
    CH = 440 if T % 440 == 0 else T // 4
    assert NB * G <= 512 and T % CH == 0 and CH <= 512 and E + P < AHEAD and NB < 256
    assert REST % G == 0 and REST > 0 and FULL == NG - 1

    def dram(name, shape, dt=F32):
        return nc.dram_tensor(name, shape, dt).ap()

    recs = dram("edges_by_dst_block", [E + P, REC])
    msgs = dram("messages_by_src_block", [E + P, MSG])
    xpad = dram("x_padded", [NBP * P, P])
    x1d = dram("x_after_layer0", [NBP * P, P])
    ytabs = [dram(f"relation_products{n}", [(NB + 1) * P, R * P]) for n in range(2)]

    def wait(e, s, value):
        if not isinstance(value, int) or value > 0:
            e.wait_ge(s, value)

    def halves(e, count, group, peel_last=False):
        for h in range(2):
            group(0, h)
        with e.Fori(1, count - peel_last) as i:
            for h in range(2):
                group(i, h)
        if peel_last:
            for h in range(2):
                group(count - 1, h)

    def staggered(e, count, first, second):
        first(0, 0)
        first(0, 1)
        second(0, 0)
        first(1, 0)
        second(0, 1)
        first(1, 1)
        second(1, 0)
        with e.Fori(2, count) as i:
            first(i, 0)
            second(i - 1, 1)
            first(i, 1)
            second(i, 0)
        second(count - 1, 1)

    def pipeline(e, count, step):
        step(None, None, (0, 0))
        step(None, (0, 0), (0, 1))
        step((0, 0), (0, 1), (1, 0))
        step((0, 1), (1, 0), (1, 1))
        step((1, 0), (1, 1), (2, 0))
        with e.Fori(2, count - 1) as i:
            step((i - 1, 1), (i, 0), (i, 1))
            step((i, 0), (i, 1), (i + 1, 0))
        i = count - 1
        step((i - 1, 1), (i, 0), (i, 1))
        step((i, 0), (i, 1), None)
        step((i, 1), None, None)

    taken = {}

    def unique(name):
        taken[name] = taken.get(name, 0) + 1
        return name if taken[name] == 1 else f"{name}_{taken[name]}"

    ctx = ExitStack()
    with ctx:
        def sb(name, shape, dt=F32, c=ctx):
            return c.enter_context(nc.sbuf_tensor(unique(name), shape, dt))

        def psum(name, shape, dt=F32, c=ctx):
            return c.enter_context(nc.psum_tensor(unique(name), shape, dt))

        counted = []

        def sem(name, c=ctx):
            counted.append(c.enter_context(nc.semaphore(unique(name))))
            return counted[-1]

        def clear(sems):
            with nc.Block() as block:

                @block.gpsimd
                def _(e):
                    for s in sems:
                        e.sem_clear(s)

        iota = sb("iota", [P, 160])
        identf = sb("identf", [P, P])
        identb = sb("identb", [P, P], BF16)
        onesf = sb("onesf", [P, P])
        onesb = sb("onesb", [P, P], BF16)
        before = sb("before", [P, P], BF16)
        notbefore = sb("notbefore", [P, P], BF16)
        maps = sb("maps", [P, T], I32)
        blk_d = sb("blk_d", [P, T])
        blk_s = sb("blk_s", [P, T])
        unsorted = sb("unsorted", [P, 1], I32)
        starts = sb("starts", [P, 2, NB])
        loc = sb("loc", [P, T])
        row = sb("row", [P, T])
        typ = sb("typ", [P, T])
        counts = sb("counts", [P, NB * R])
        wgt = sb("wgt", [P, T])
        s_passed = {eng.engine: sem(f"passed_{n}") for n, eng in
                    enumerate((nc.vector, nc.scalar, nc.tensor, nc.gpsimd, nc.sync))}

        def settle(e):
            e.sem_inc(s_passed[e.engine], 1)

        def tile_values(e, lane, first, most, count=G):
            _, values = nc.values_load_multi_w_load_instructions(
                maps[lane:lane + 1, bass.ds(first, count)], engines=[e.engine], min_val=0, max_val=most,
                skip_runtime_bounds_check_because="the tile maps are clamped to this range")
            return values

        def over_groups(ap, width):
            return ap.unsqueeze(1).broadcast_to([ap.shape[0], G, width])

        def over_width(ap, width):
            return ap.unsqueeze(2).broadcast_to([ap.shape[0], G, width])


        sorting = ExitStack()
        keep = sb("keep", [P, max(TE * AUX, CHUNKS * G * P)], c=sorting)
        aux = keep[:, 0:TE * AUX].rearrange("p (t f) -> p t f", f=AUX)
        dkey = sb("dkey", [P, TE], BF16, sorting)
        skey = sb("skey", [P, TE], BF16, sorting)
        with ExitStack() as c:
            kint = sb("kint", [CR, 3, CHUNKS, G * P], I32, c)
            bint = sb("bint", [CR, CHUNKS, G * P], I32, c)
            fld = sb("fld", [CR, 6, CHUNKS, G * P], c=c)
            cnt = sb("cnt", [P, 2, NB], c=c)
            num = sb("num", [P, 2, NB + 1], c=c)
            numi = sb("numi", [P, 2, NB + 1], I32, c)
            til = sb("til", [P, 2, NB + 1], c=c)
            zero = sb("zero", [P, NB], c=c)
            tend = sb("tend", [P, 2, NB], c=c)
            nend = sb("nend", [P, 2, NB], c=c)
            tcol = sb("tcol", [P, 2], c=c)
            slack = sb("slack", [P, 2], c=c)
            slackb = sb("slackb", [P, 2, P], BF16, c)
            iotat = sb("iotat", [P, T], c=c)
            past = sb("past", [P, 2, T], BF16, c)
            junk = past[:, :, 0:TE]
            ps_row = psum("ps_row", [P, 2, NB], c=c)
            ps_col = psum("ps_col", [P, 4], c=c)
            ps_b = psum("ps_b", [P, CH], c=c)
            ps_o = psum("ps_o", [P, CH], c=c)
            offs = sb("offs", [P, CH], c=c)
            s_pad, s_in, s_pool, s_v = sem("pads_set", c), sem("keys_loaded", c), sem("pool_consts", c), sem("dve_step", c)
            s_cnt, s_num, s_tend, s_tcol = sem("counted", c), sem("numbers", c), sem("tile_ends", c), sem("tile_ends_col", c)
            s_past, s_map, s_mapd = sem("past_ready", c), sem("map_products", c), sem("map_done", c)
            nxt = keep[0:CR, 0:CHUNKS * G * P].bitcast(I32)\
                .rearrange("p (c q) -> p c q", c=CHUNKS)
            viol = sb("viol", [P, 1], c=c)
            ps_u = psum("ps_u", [P, 1], c=c)
            s_viol, s_up = sem("violations_ready", c), sem("violations_summed", c)
            s_fld, s_tr, s_ev = sem("fields_ready", c), sem("fields_turned", c), sem("fields_copied", c)
            ps_t = psum("ps_t", [P, 2, 512], c=c)
            with nc.Block() as block:

                @block.sync
                def _(e):
                    e.wait_ge(s_pad, 3)
                    for n, a in enumerate((dst, src, edge_type, edge_weight)):
                        to = kint[:, n] if n < 3 else fld[:, CUT - WORDS]
                        full = a[0:FULL * G * P].rearrange("(c q) -> c q", q=G * P)
                        for ch in range(CHUNKS):
                            rows = min(CR, FULL - ch * CR)
                            e.dma_start(to[0:rows, ch, :], full[ch * CR:ch * CR + rows, :]).then_inc(s_in, 16)
                        e.dma_start(to[CR - 1:CR, CHUNKS - 1, 0:REST],
                                    a[FULL * G * P:E].rearrange("(p t) -> p t", p=1)).then_inc(s_in, 16)
                    later = dst[1:1 + FULL * G * P].rearrange("(c q) -> c q", q=G * P)
                    for ch in range(CHUNKS):
                        rows = min(CR, FULL - ch * CR)
                        e.dma_start(nxt[0:rows, ch, :], later[ch * CR:ch * CR + rows, :]).then_inc(s_in, 16)
                    e.dma_start(nxt[CR - 1:CR, CHUNKS - 1, 0:REST - 1],
                                dst[FULL * G * P + 1:E].rearrange("(p t) -> p t", p=1)).then_inc(s_in, 16)

                @block.gpsimd
                def _(e):
                    e.iota(iota[:, :], [[1, 160]], base=0, channel_multiplier=0,
                           allow_small_or_imprecise_dtypes=True).then_inc(s_pool, 1)
                    e.iota(iotat[:, :], [[1, T]], base=0, channel_multiplier=0,
                           allow_small_or_imprecise_dtypes=True).then_inc(s_pool, 1)
                    e.memset(identf[:, :], 0.0).then_inc(s_pool, 1)
                    e.memset(onesf[:, :], 1.0).then_inc(s_pool, 1)
                    e.memset(onesb[:, :], 1.0).then_inc(s_pool, 1)
                    e.wait_ge(s_pool, 5)
                    e.affine_select(out=identf[:, :], in_=identf[:, :], compare_op=ALU.not_equal, fill=1.0,
                                    base=0, pattern=[[-1, P]], channel_multiplier=1).then_inc(s_pool, 1)
                    e.affine_select(out=before[:, :], in_=onesb[:, :], compare_op=ALU.is_gt, fill=0.0,
                                    base=0, pattern=[[1, P]], channel_multiplier=-1).then_inc(s_pool, 1)
                    e.affine_select(out=notbefore[:, :], in_=onesb[:, :], compare_op=ALU.is_ge, fill=0.0,
                                    base=0, pattern=[[-1, P]], channel_multiplier=1).then_inc(s_pool, 1)

                @block.vector
                def _(e):
                    steps = [0]

                    def then_wait(ins):
                        steps[0] += 1
                        ins.then_inc(s_v, 1)
                        e.wait_ge(s_v, steps[0])

                    e.memset(kint[:, :, :, :], -1).then_inc(s_pad, 1)
                    e.memset(fld[:, CUT - WORDS, :, :], 0.0).then_inc(s_pad, 1)
                    e.memset(nxt[:, :, :], NB * P).then_inc(s_pad, 1)
                    e.memset(viol[:, :], 0.0)
                    e.memset(zero[:, :], 0.0)
                    then_wait(e.memset(num[:, :, :], 0.0))
                    e.wait_ge(s_pool, 8)
                    e.tensor_copy(identb[:, :], identf[:, :])
                    e.wait_ge(s_in, 16 * 5 * (CHUNKS + 1))
                    then_wait(e.tensor_scalar(bint[:, :, :], kint[:, 1], 7, None, ALU.arith_shift_right))
                    then_wait(e.tensor_scalar(fld[:, SBLK - WORDS], bint[:, :, :], 1.0, None, ALU.add))
                    then_wait(e.tensor_scalar(bint[:, :, :], kint[:, 0], 7, None, ALU.arith_shift_right))
                    e.tensor_copy(fld[:, 5], bint[:, :, :])
                    e.tensor_copy(fld[:, DST - WORDS], kint[:, 0])
                    e.tensor_copy(fld[:, SRC - WORDS], kint[:, 1])
                    e.scalar_tensor_tensor(out=fld[:, ROW - WORDS], in0=kint[:, 1], scalar=float(R),
                                           in1=kint[:, 2], op0=ALU.mult, op1=ALU.add).then_inc(s_fld, 1)
                    e.wait_ge(s_fld, 1)
                    then_wait(e.tensor_scalar(bint[:, :, :], nxt[:, :, :], 7, None, ALU.arith_shift_right))
                    then_wait(e.tensor_tensor(nxt[:, :, :], fld[:, 5], bint[:, :, :], ALU.is_gt))
                    e.tensor_reduce(viol[0:CR, :], nxt[:, :, :].rearrange("p a b -> p (a b)"), AX, ALU.max)\
                     .then_inc(s_viol, 1)
                    e.wait_ge(s_viol, 1)
                    done = 0
                    for f in range(6):
                        for ch in range(CHUNKS):
                            done += 1
                            e.wait_ge(s_tr, done)
                            turned = ps_t[:, done % 2, 0:G * CR].rearrange("p (k c) -> p c k", k=G)
                            if f < 5:
                                e.tensor_copy(aux[:, ch * CR * G:(ch + 1) * CR * G, f].rearrange("p (c k) -> p c k", k=G),
                                              turned).then_inc(s_ev, 1)
                            else:
                                e.tensor_copy(dkey[:, ch * CR * G:(ch + 1) * CR * G].rearrange("p (c k) -> p c k", k=G),
                                              turned).then_inc(s_ev, 1)
                    e.wait_ge(s_ev, done)
                    then_wait(e.tensor_copy(skey[:, :], aux[:, :, SBLK - WORDS]))
                    for b in range(NB):
                        wait(e, s_cnt, 2 * b - 1)
                        e.tensor_scalar(junk[:, 0], dkey[:, :], float(b), None, ALU.is_equal, ALU.add,
                                        accum_out=cnt[:, 0, b:b + 1]).then_inc(s_cnt, 1)
                        wait(e, s_cnt, 2 * b)
                        e.tensor_scalar(junk[:, 1], skey[:, :], float(b + 1), None, ALU.is_equal, ALU.add,
                                        accum_out=cnt[:, 1, b:b + 1]).then_inc(s_cnt, 1)
                    e.wait_ge(s_up, 1)
                    e.tensor_copy(unsorted[:, :], ps_u[:, :])
                    e.wait_ge(s_num, 1)
                    e.tensor_copy(num[:, :, 0:NB], ps_row[:, :, :])
                    then_wait(e.tensor_copy(num[0:NB, :, NB], ps_col[0:NB, 0:2]))
                    then_wait(e.tensor_scalar(numi[:, :, :], num[:, :, :], float(P - 1), None, ALU.add))
                    then_wait(e.tensor_scalar(numi[:, :, :], numi[:, :, :], 7, None, ALU.arith_shift_right))
                    then_wait(e.tensor_copy(til[:, :, :], numi[:, :, :]))
                    for n in range(2):
                        e.tensor_tensor_scan(tend[:, n, :], til[:, n, 0:NB], zero[:, :], 0.0, ALU.add, ALU.add)
                        then_wait(e.tensor_tensor_scan(nend[:, n, :], num[:, n, 0:NB], zero[:, :], 0.0,
                                                       ALU.add, ALU.add))
                    then_wait(e.tensor_tensor(starts[:, :, :], nend[:, :, :], num[:, :, 0:NB], ALU.subtract))
                    e.tensor_scalar(starts[:, :, :], starts[:, :, :], -AHEAD, None, ALU.add)
                    then_wait(e.scalar_tensor_tensor(out=slack[:, :], in0=til[:, :, NB], scalar=-float(P),
                                                     in1=num[:, :, NB], op0=ALU.mult, op1=ALU.add))
                    for n in range(2):
                        ins = e.tensor_scalar(slackb[:, n, :], onesb[:, :], slack[:, n:n + 1], None, ALU.mult)
                    ins.then_inc(s_tend, 1)
                    e.wait_ge(s_tcol, 1)
                    then_wait(e.tensor_copy(tcol[0:NB, :], ps_col[0:NB, 2:4]))
                    for n in range(2):
                        ins = e.tensor_scalar(past[0:NB, n, :], iotat[0:NB, :], tcol[0:NB, n:n + 1], None, ALU.is_ge)
                    ins.then_inc(s_past, 1)
                    done = 0
                    for n in range(2):
                        blk = (blk_d, blk_s)[n]
                        for q in range(0, T, CH):
                            done += 1
                            e.wait_ge(s_map, done)
                            e.tensor_scalar(blk[:, q:q + CH], ps_b[:, :], float(NB - 1), float(P), ALU.min, ALU.mult)
                            e.tensor_scalar(maps[64 * n:64 * n + 32, q:q + CH], ps_b[64 * n:64 * n + 32, :],
                                            float(NB - 1), float(R), ALU.min, ALU.mult)
                            then_wait(e.scalar_tensor_tensor(out=offs[:, :], in0=iotat[:, q:q + CH], scalar=float(P),
                                                             in1=ps_o[:, :], op0=ALU.mult, op1=ALU.add))
                            lane = 64 * n + 32
                            e.tensor_scalar(maps[lane:lane + 32, q:q + CH], offs[lane:lane + 32, :],
                                            float(E), None, ALU.min).then_inc(s_mapd, 1)
                            e.wait_ge(s_mapd, done)

                @block.tensor
                def _(e):
                    e.wait_ge(s_fld, 1)
                    e.wait_ge(s_pool, 8)
                    e.wait_ge(s_viol, 1)
                    e.matmul(ps_u[:, :], onesf[:, :], viol[:, :], start=True, stop=True).then_inc(s_up, 1)
                    done = 0
                    for f in range(6):
                        for ch in range(CHUNKS):
                            done += 1
                            wait(e, s_ev, done - 2)
                            lanes = fld[:, f, ch, :].rearrange("c (p k) -> c k p", k=G)
                            for k in range(G):
                                mm = e.transpose(ps_t[:, done % 2, k * CR:(k + 1) * CR], lanes[:, k, :],
                                                 identf[0:CR, 0:CR])
                            mm.then_inc(s_tr, 1)
                    e.wait_ge(s_cnt, 2 * NB)
                    for n in range(2):
                        e.matmul(ps_row[:, n, :], onesf[:, :], cnt[:, n, :], start=True, stop=True)
                        mm = e.matmul(ps_col[0:NB, n:n + 1], cnt[:, n, :], onesf[:, 0:1], start=True, stop=True)
                    mm.then_inc(s_num, 1)
                    e.wait_ge(s_tend, 1)
                    for n in range(2):
                        mm = e.matmul(ps_col[0:NB, 2 + n:3 + n], tend[0:1, n, :], onesf[0:1, 0:1], start=True, stop=True)
                    mm.then_inc(s_tcol, 1)
                    e.wait_ge(s_past, 1)
                    done = 0
                    for n in range(2):
                        for q in range(0, T, CH):
                            wait(e, s_mapd, done)
                            e.matmul(ps_b[:, :], onesb[0:NB, :], past[0:NB, n, q:q + CH], start=True, stop=True)
                            e.matmul(ps_o[:, :], slackb[0:NB, n, :], past[0:NB, n, q:q + CH], start=True, stop=True)\
                             .then_inc(s_map, 1)
                            done += 1

        clear(counted[len(s_passed):])

        def rank_start(e, ranks, n):
            e.matmul(ranks[:, :, :], onesf[0:1, :], starts[0:1, n, :].unsqueeze(1).broadcast_to([1, RG, NB]),
                     start=True, stop=True, skip_group_check=True)

        def rank_before(e, ranks, hot, at):
            e.matmul(ranks[:, :, :], before[:, :], hot[:, at:at + RG, :], start=False, stop=True,
                     skip_group_check=True)
            return e.matmul(ranks[:, 1, :], onesb[:, :], hot[:, at, :], start=False, stop=True,
                            skip_group_check=True)

        def rank_after(e, ranks, hot, at):
            e.matmul(ranks[:, :, :], notbefore[:, :], hot[:, at:at + RG, :], start=False, stop=True,
                     skip_group_check=True)
            return e.matmul(ranks[:, 0, :], onesb[:, :], hot[:, at + 1, :], start=False, stop=True,
                            skip_group_check=True)

        with sorting, ExitStack() as c:
            hot = [sb(f"hot{h}", [P, G, NB], BF16, c) for h in range(2)]
            rank = sb("rank", [P, G, NB], c=c)
            posf = [sb(f"posf{h}", [P, G], c=c) for h in range(2)]
            pos = [sb(f"pos{h}", [P, G], I32, c) for h in range(2)]
            fin = [sb(f"fin{h}", [P, WIDE, G, NRBF], c=c) for h in range(2)]
            rest = [sb(f"rest{h}", [P, WIDE * G, NRBF], c=c) for h in range(2)]
            rec = [sb(f"rec{h}", [P, WIDE * G, REC], c=c) for h in range(2)]
            tail = sb("tail", [P, MSG], c=c)
            ranks = psum("ranks", [P, RG, NB], c=c)
            stacks = [rec[h][:, :, 0:WORDS].bitcast(BF16) for h in range(2)]
            s_f = [sem(f"basis_loaded{h}", c) for h in range(2)]
            s_sc = [sem(f"records_stored{h}", c) for h in range(2)]
            s_out = [sem(f"wide_records_stored{h}", c) for h in range(2)]
            s_hi, s_r1, s_mid, s_rec = sem("high_parts", c), sem("first_rests", c), sem("middle_parts", c), sem("records_built", c)
            s_low = sem("low_parts", c)
            s_hot, s_before, s_read = sem("hot_built", c), sem("ranks_ready", c), sem("ranks_read", c)
            s_red, s_pos, s_after = sem("ranks_summed", c), sem("positions_ready", c), sem("ranks_moved", c)
            s_tail, s_tout = sem("tail_set", c), sem("tail_stored", c)

            def split_act(e, g, h, tiles, first, stored, was):
                n = tiles
                e.wait_ge(*first)
                wait(e, stored, was)
                f = fin[h][:, :, :, :].rearrange("p w k f -> p (w k) f")[:, 0:n, :]
                hi = stacks[h][:, 0:n, 0:3 * NRBF].rearrange("p n (s f) -> p n s f", s=3)
                mid = stacks[h][:, 0:n, 3 * NRBF:5 * NRBF].rearrange("p n (s f) -> p n s f", s=2)
                e.activation(hi, f.unsqueeze(2).broadcast_to([P, n, 3, NRBF]), ACT.Copy).then_inc(s_hi, 1)
                settle(e)
                e.activation(rec[h][:, 0:n, WORDS:REC], aux[:, bass.ds(g * n, n), :], ACT.Copy).then_inc(s_rec, 1)
                e.wait_ge(s_r1, g + 1)
                e.activation(mid, rest[h][:, 0:n, :].unsqueeze(2).broadcast_to([P, n, 2, NRBF]), ACT.Copy).then_inc(s_mid, 1)

            def split_dve(e, g, h, tiles):
                n = tiles
                f = fin[h][:, :, :, :].rearrange("p w k f -> p (w k) f")[:, 0:n, :]
                e.wait_ge(s_hi, g + 1)
                wait(e, s_low, g - 1)
                e.tensor_tensor(rest[h][:, 0:n, :], f, stacks[h][:, 0:n, 0:NRBF], ALU.subtract).then_inc(s_r1, 1)
                e.wait_ge(s_mid, g + 1)
                e.tensor_tensor(stacks[h][:, 0:n, 5 * NRBF:6 * NRBF], rest[h][:, 0:n, :],
                                stacks[h][:, 0:n, 3 * NRBF:4 * NRBF], ALU.subtract).then_inc(s_low, 1)

            with nc.Block() as block:

                @block.sync
                def _(e):
                    e.wait_ge(s_tail, 1)
                    e.dma_start(recs[E:E + P, :], tail[:, 0:REC]).then_inc(s_tout, 16)
                    e.dma_start(msgs[E:E + P, :], tail[:, :]).then_inc(s_tout, 16)
                    e.wait_ge(s_tail, 4)

                    def by_group(i, h):
                        wait(e, s_low, 2 * i + h - 1)
                        lanes = REST // G if isinstance(i, int) and 2 * i + h == NG - 1 else P
                        e.dma_start(fin[h][0:lanes, 0, :, :],
                                    edge_attr[bass.ds((2 * i + h) * (G * P), lanes * G), :]
                                    .rearrange("(p k) f -> p k f", k=G)).then_inc(s_f[h], 16)

                    def wide_load(i, h):
                        wait(e, s_low, 2 * i + h - 1)
                        at = (2 * i + h) * (WIDE * G * P)
                        whole = WIDE - 1 if isinstance(i, int) and 2 * i + h == NG // WIDE - 1 else WIDE
                        if whole:
                            e.dma_start(fin[h][:, 0:whole, :, :].rearrange("p w k f -> p w (k f)"),
                                        edge_attr[bass.ds(at, whole * G * P), :].rearrange("n f -> (n f)")
                                        .rearrange("(w p q) -> p w q", p=P, q=G * NRBF)).then_inc(s_f[h], 16)
                        lanes = REST // G if whole < WIDE else P
                        if whole < WIDE:
                            e.dma_start(fin[h][0:lanes, whole, :, :],
                                        edge_attr[FULL * G * P:E, :].rearrange("(p k) f -> p k f", k=G)).then_inc(s_f[h], 16)

                    def wide_store(i, h):
                        g = 2 * i + h
                        e.wait_ge(s_low, g + 1)
                        e.wait_ge(s_rec, g + 1)
                        whole = WIDE - 1 if isinstance(i, int) and g == NG // WIDE - 1 else WIDE
                        rows = recs[bass.ds(g * (WIDE * G * P), whole * G * P), :]
                        if whole:
                            e.dma_start(rows.rearrange("n f -> (n f)").rearrange("(w p q) -> p w q", p=P, q=G * REC),
                                        rec[h][:, 0:whole * G, :].rearrange("p (w k) f -> p w (k f)", k=G)).then_inc(s_out[h], 16)
                        if whole < WIDE:
                            e.dma_start(recs[FULL * G * P:E, :].rearrange("(p k) f -> p k f", k=G),
                                        rec[h][0:REST // G, whole * G:WIDE * G, :]).then_inc(s_out[h], 16)

                    def wide(last, this, coming):
                        if coming:
                            wide_load(*coming)
                        if last:
                            wide_store(*last)

                    out_of_order = e.value_load(unsorted[0:1, 0:1], min_val=0, max_val=P)
                    with e.If(out_of_order > 0):
                        halves(e, HALF_E, by_group, peel_last=True)
                    with e.Else():
                        pipeline(e, HALF_E // WIDE, wide)
                        e.wait_ge(s_out[0], 16 * (HALF_E // WIDE))
                        e.wait_ge(s_out[1], 16 * (HALF_E // WIDE + (WIDE > 1)))
                    e.wait_ge(s_tout, 32)

                @block.vector
                def _(e):
                    e.memset(tail[:, :], -1.0).then_inc(s_tail, 1)
                    for h in range(2):
                        e.memset(stacks[h][:, :, ONES:2 * WORDS], 1.0).then_inc(s_tail, 1)
                        ins = e.memset(fin[h][:, :, :, :], 0.0)
                    ins.then_inc(s_tail, 1)

                    def by_group(i, h):
                        g = 2 * i + h
                        wait(e, s_after, 2 * (g - 1))
                        e.tensor_tensor(hot[h][:, :, :], over_groups(iota[:, 0:NB], NB),
                                        over_width(dkey[:, bass.ds(g * G, G)], NB), ALU.is_equal).then_inc(s_hot, 1)
                        split_dve(e, g, h, G)
                        wait(e, s_red, g)
                        for r in range(0, G, RG):
                            e.wait_ge(s_before, 2 * g + r // RG + 1)
                            e.tensor_tensor(rank[:, r:r + RG, :], ranks[:, :, :], hot[h][:, r:r + RG, :], ALU.mult)\
                             .then_inc(s_read, 1)
                        e.wait_ge(s_read, 2 * g + 2)
                        e.tensor_reduce(posf[h][:, :], rank[:, :, :], AX, ALU.add).then_inc(s_red, 1)
                        e.wait_ge(s_red, g + 1)
                        wait(e, s_sc[h], i * (16 * G))
                        e.tensor_scalar(pos[h][:, :], posf[h][:, :], AHEAD, None, ALU.add).then_inc(s_pos, 1)

                    def wide(i, h):
                        split_dve(e, 2 * i + h, h, WIDE * G)

                    out_of_order = e.value_load(unsorted[0:1, 0:1], min_val=0, max_val=P)
                    with e.If(out_of_order > 0):
                        halves(e, HALF_E, by_group)
                    with e.Else():
                        halves(e, HALF_E // WIDE, wide)

                @block.tensor
                def _(e):
                    def by_group(i, h):
                        g = 2 * i + h
                        e.wait_ge(s_hot, g + 1)
                        for r in range(0, G, RG):
                            rank_before(e, ranks, hot[h], r).then_inc(s_before, 1)
                            e.wait_ge(s_read, 2 * g + r // RG + 1)
                            rank_after(e, ranks, hot[h], r).then_inc(s_after, 1)

                    out_of_order = e.value_load(unsorted[0:1, 0:1], min_val=0, max_val=P)
                    with e.If(out_of_order > 0):
                        rank_start(e, ranks, 0)
                        halves(e, HALF_E, by_group)
                    with e.Else():
                        pass

                @block.scalar
                def _(e):
                    def by_group(i, h):
                        split_act(e, 2 * i + h, h, G, (s_f[h], 16 * (i + 1)), s_sc[h], i * (16 * G))

                    def wide(i, h):
                        last = WIDE > 1 and isinstance(i, int) and 2 * i + h == NG // WIDE - 1
                        split_act(e, 2 * i + h, h, WIDE * G, (s_f[h], 16 * (i + 1 + last)), s_out[h], 16 * i)

                    e.wait_ge(s_tail, 4)
                    out_of_order = e.value_load(unsorted[0:1, 0:1], min_val=0, max_val=P)
                    with e.If(out_of_order > 0):
                        halves(e, HALF_E, by_group)
                    with e.Else():
                        halves(e, HALF_E // WIDE, wide, peel_last=True)

                @block.gpsimd
                def _(e):
                    def by_group(i, h):
                        g = 2 * i + h
                        e.wait_ge(s_rec, g + 1)
                        e.wait_ge(s_low, g + 1)
                        e.wait_ge(s_pos, g + 1)
                        settle(e)
                        for k in range(G):
                            e.indirect_dma_start(
                                out=recs, out_offset=bass.IndirectOffsetOnAxis(ap=pos[h][:, k:k + 1], axis=0),
                                in_=rec[h][:, k, :], in_offset=None, bounds_check=E - 1, oob_is_err=False)\
                             .then_inc(s_sc[h], 16)

                    out_of_order = e.value_load(unsorted[0:1, 0:1], min_val=0, max_val=P)
                    with e.If(out_of_order > 0):
                        halves(e, HALF_E, by_group)
                        for h in range(2):
                            e.wait_ge(s_sc[h], HALF_E * 16 * G)
                    with e.Else():
                        pass

        messages = ExitStack()
        hf = sb("hf", [P, NB, 3, P], BF16, messages)
        with ExitStack() as c:
            xs = sb("xs", [P, NBP, P], c=c)
            mean = sb("mean", [P, NBP], c=c)
            var = sb("var", [P, NBP], c=c)
            std = sb("std", [P, NBP], c=c)
            rstd = sb("rstd", [P, NBP], c=c)
            win = sb("win", [P, P], c=c)
            sq = [sb(f"sq{h}", [P, G, P], c=c) for h in range(2)]
            hn = [sb(f"hn{h}", [P, G, P], c=c) for h in range(2)]
            hT = [sb(f"hT{h}", [P, G, P], c=c) for h in range(2)]
            left = [sb(f"left{h}", [P, G, P], c=c) for h in range(2)]
            ps_tr = [psum(f"ps_tr{h}", [P, G, P], c=c) for h in range(2)]
            ps_hf = [psum(f"ps_hf{h}", [P, G, P], c=c) for h in range(2)]
            s_sq, s_sum, s_cen = sem("squares_ready", c), sem("squares_summed", c), sem("x_centered", c)
            s_in, s_set, s_out = sem("x_loaded", c), sem("x_pad_set", c), sem("x_stored", c)
            s_v, s_var, s_std = sem("dve_step", c), sem("variances_ready", c), sem("std_ready", c)
            s_hn, s_tr, s_hT, s_hf = sem("h_ready", c), sem("h_turned", c), sem("hT_ready", c), sem("hf_ready", c)
            s_hi, s_mid, s_lo = sem("high_part", c), sem("middle_part", c), sem("low_part", c)
            s_sub = sem("rest_ready", c)
            NGR = NBP // G
            with nc.Block() as block:

                @block.sync
                def _(e):
                    e.dma_start(win[:, :], w_in).then_inc(s_in, 16)
                    e.wait_ge(s_set, 1)
                    e.dma_start(xs[:, 0:NB - 1, :], x[0:(NB - 1) * P, :].rearrange("(m p) f -> p m f", p=P)).then_inc(s_in, 16)
                    e.dma_start(xs[0:LAST, NB - 1, :], x[(NB - 1) * P:N, :]).then_inc(s_in, 16)
                    e.wait_ge(s_in, 48)
                    e.dma_start(xpad.rearrange("(m p) f -> p m f", p=P), xs[:, :, :]).then_inc(s_out, 16)
                    e.wait_ge(s_out, 16)

                def blocks(n):
                    return min(G, NB - n * G)

                def part(n, p):
                    return hf[:, n * G:n * G + blocks(n), p, :]

                @block.vector
                def _(e):
                    steps = [0]

                    def then_wait(ins):
                        steps[0] += 1
                        ins.then_inc(s_v, 1)
                        e.wait_ge(s_v, steps[0])

                    e.memset(xs[:, NB - 1:NBP, :], 0.0).then_inc(s_set, 1)
                    e.wait_ge(s_in, 48)
                    then_wait(e.tensor_reduce(mean[:, :], xs[:, :, :], AX, ALU.add))
                    then_wait(e.tensor_scalar(mean[:, :], mean[:, :], 1.0 / P, None, ALU.mult))
                    e.wait_ge(s_out, 16)
                    for n in range(NGR):
                        rows = slice(n * G, (n + 1) * G)
                        e.tensor_tensor(xs[:, rows, :], xs[:, rows, :], over_width(mean[:, rows], P), ALU.subtract)\
                         .then_inc(s_cen, 1)
                    for n in range(NGR):
                        e.wait_ge(s_sq, n + 1)
                        e.tensor_reduce(var[:, n * G:(n + 1) * G], sq[n % 2][:, :, :], AX, ALU.add).then_inc(s_sum, 1)
                    e.wait_ge(s_sum, NGR)
                    e.tensor_scalar(var[:, :], var[:, :], 1.0 / P, EPS, ALU.mult, ALU.add).then_inc(s_var, 1)
                    e.wait_ge(s_std, 1)
                    then_wait(e.reciprocal(rstd[:, :], std[:, :]))
                    for n in range(NGR + 3):
                        if n < NGR:
                            wait(e, s_tr, n - 1)
                            e.tensor_tensor(hn[n % 2][:, :, :], xs[:, n * G:(n + 1) * G, :],
                                            over_width(rstd[:, n * G:(n + 1) * G], P), ALU.mult).then_inc(s_hn, 1)
                        if 2 <= n < NGR + 2:
                            m = n - 2
                            e.wait_ge(s_hi, m + 1)
                            wait(e, s_lo, m - 1)
                            e.tensor_tensor(left[m % 2][:, 0:blocks(m), :], ps_hf[m % 2][:, 0:blocks(m), :], part(m, HIGH),
                                            ALU.subtract).then_inc(s_sub, 1)
                        if n >= 3:
                            m = n - 3
                            e.wait_ge(s_mid, m + 1)
                            e.tensor_tensor(part(m, LOW), left[m % 2][:, 0:blocks(m), :], part(m, MID), ALU.subtract)\
                             .then_inc(s_lo, 1)

                @block.scalar
                def _(e):
                    for n in range(NGR):
                        e.wait_ge(s_cen, n + 1)
                        wait(e, s_sum, n - 1)
                        e.activation(sq[n % 2][:, :, :], xs[:, n * G:(n + 1) * G, :], ACT.Square).then_inc(s_sq, 1)
                    e.wait_ge(s_var, 1)
                    e.activation(std[:, :], var[:, :], ACT.Sqrt).then_inc(s_std, 1)
                    for n in range(NGR + 2):
                        if n < NGR:
                            e.wait_ge(s_tr, n + 1)
                            wait(e, s_hf, n - 1)
                            e.activation(hT[n % 2][:, :, :], ps_tr[n % 2][:, :, :], ACT.Relu).then_inc(s_hT, 1)
                        if 1 <= n <= NGR:
                            m = n - 1
                            e.wait_ge(s_hf, m + 1)
                            e.activation(part(m, HIGH), ps_hf[m % 2][:, 0:blocks(m), :], ACT.Copy).then_inc(s_hi, 1)
                        if n >= 2:
                            m = n - 2
                            e.wait_ge(s_sub, m + 1)
                            e.activation(part(m, MID), left[m % 2][:, 0:blocks(m), :], ACT.Copy).then_inc(s_mid, 1)

                @block.tensor
                def _(e):
                    e.wait_ge(s_in, 48)
                    for n in range(NGR + 1):
                        if n < NGR:
                            e.wait_ge(s_hn, n + 1)
                            wait(e, s_hT, n - 1)
                            for k in range(G):
                                mm = e.transpose(ps_tr[n % 2][:, k, :], hn[n % 2][:, k, :], identf[:, :])
                            mm.then_inc(s_tr, 1)
                        if n:
                            m = n - 1
                            e.wait_ge(s_hT, m + 1)
                            wait(e, s_sub, m - 1)
                            for k in range(G):
                                mm = e.matmul(ps_hf[m % 2][:, k, :], hT[m % 2][:, k, :], win[:, :], start=True, stop=True)
                            mm.then_inc(s_hf, 1)

        with messages, ExitStack() as c:
            rec = [sb(f"rec{h}", [P, G, REC], c=c) for h in range(2)]
            stacks = [rec[h][:, :, 0:WORDS].bitcast(BF16) for h in range(2)]
            late = [sb(f"late{h}", [P, G, AUX], c=c) for h in range(2)]
            skey = [sb(f"skey{h}", [P, G], c=c) for h in range(2)]
            here = [sb(f"here{h}", [P, G], c=c) for h in range(2)]
            kind = [sb(f"kind{h}", [P, G], c=c) for h in range(2)]
            hot = [sb(f"hot{h}", [P, G, NB], BF16, c) for h in range(2)]
            node = [sb(f"node{h}", [P, G, P], BF16, c) for h in range(2)]
            nodeT = [sb(f"nodeT{h}", [P, G, P], BF16, c) for h in range(2)]
            hott = [sb(f"hott{h}", [P, G, R], BF16, c) for h in range(2)]
            rank = sb("rank", [P, G, NB], c=c)
            posf = [sb(f"posf{h}", [P, G], c=c) for h in range(2)]
            srcs = [sb(f"srcs{h}", [P, G, 1], c=c) for h in range(2)]
            pos = [sb(f"pos{h}", [P, G], I32, c) for h in range(2)]
            fT = [sb(f"fT{h}", [KF, G * P], BF16, c) for h in range(2)]
            soft = [sb(f"soft{h}", [P, G * P], c=c) for h in range(2)]
            filt = [sb(f"filt{h}", [P, G, P], c=c) for h in range(2)]
            hcut = [sb(f"hcut{h}", [P, G, P], c=c) for h in range(2)]
            msg = [sb(f"msg{h}", [P, G, MSG], c=c) for h in range(2)]
            wf1 = sb("wf1", [NRBF + 1, P], c=c)
            wparts = sb("wparts", [NRBF + 1, 3, P], BF16, c)
            wstack = sb("wstack", [KF, P], BF16, c)
            wf2 = sb("wf2", [P, P], c=c)
            bf2 = sb("bf2", [1, P], c=c)
            bparts = sb("bparts", [1, 3, P], BF16, c)
            brows = sb("brows", [3, G, P], BF16, c)
            half = sb("half", [P, 1], c=c)
            ranks = psum("ranks", [P, RG, NB], c=c)
            ps_f = psum("ps_f", [P, G * P], BF16, c)
            ps_v = [psum(f"ps_v{h}", [P, G * P], c=c) for h in range(2)]
            ps_w = psum("ps_w", [P, G, P], c=c)
            ps_g = psum("ps_g", [P, G, P], c=c)
            ps_n = psum("ps_n", [P, G, P], BF16, c)
            ps_c = psum("ps_c", [P, G, R], c=c)
            s_w, s_set, s_parts = sem("weights_loaded", c), sem("constants_set", c), sem("weight_parts", c)
            s_stack = sem("weights_stacked", c)
            s_rec = [sem(f"records_loaded{h}", c) for h in range(2)]
            s_msg = [sem(f"messages_stored{h}", c) for h in range(2)]
            s_loc, s_typ, s_key, s_late = sem("local_dst", c), sem("types", c), sem("src_keys", c), sem("late_fields", c)
            s_hot, s_node, s_hott = sem("hot_built", c), sem("node_hot_built", c), sem("type_hot_built", c)
            s_before, s_read, s_red = sem("ranks_ready", c), sem("ranks_read", c), sem("ranks_summed", c)
            s_pos, s_after = sem("positions_ready", c), sem("ranks_moved", c)
            s_fp, s_fT, s_vp = sem("basis_turned", c), sem("basis_copied", c), sem("filter1_product", c)
            s_abs, s_exp, s_log, s_filt = sem("abs", c), sem("exp", c), sem("log", c), sem("softplus_ready", c)
            s_np, s_nT, s_g, s_hc = sem("node_hot_turned", c), sem("node_hotT_copied", c), sem("hf_gathered", c), sem("hf_scaled", c)
            s_c, s_cadd = sem("type_counts", c), sem("counts_added", c)
            s_wp, s_m, s_tab = sem("filter2_product", c), sem("messages_ready", c), sem("tables_written", c)
            s_src, s_srcs = sem("message_src", c), sem("src_kept", c)
            with nc.Block() as block:

                @block.sync
                def _(e):
                    e.dma_start(wf1[0:NRBF, :], w_f1).then_inc(s_w, 16)
                    e.dma_start(wf1[NRBF:NRBF + 1, :], b_f1.rearrange("(a f) -> a f", a=1)).then_inc(s_w, 16)
                    e.dma_start(wf2[:, :], w_f2).then_inc(s_w, 16)
                    e.dma_start(bf2[:, :], b_f2.rearrange("(a f) -> a f", a=1)).then_inc(s_w, 16)
                    e.wait_ge(s_parts, 10)
                    for n, (_, part) in enumerate(STACK):
                        e.dma_start(wstack[n * NRBF:(n + 1) * NRBF, :], wparts[0:NRBF, part, :]).then_inc(s_stack, 16)
                    for part in range(3):
                        e.dma_start(wstack[ONES + part:ONES + part + 1, :], wparts[NRBF:NRBF + 1, part, :]).then_inc(s_stack, 16)
                        e.dma_start(brows[part:part + 1, :, :],
                                    bparts[:, part, :].unsqueeze(1).broadcast_to([1, G, P])).then_inc(s_stack, 16)

                    def group(i, h):
                        g = 2 * i + h
                        wait(e, s_fp, g - 1)
                        wait(e, s_late, g - 1)
                        wait(e, s_key, g - 1)
                        wait(e, s_typ, g - 1)
                        first = tile_values(e, 32, g * G, E)
                        for k in range(G):
                            e.dma_start(rec[h][:, k, :], recs[bass.ds(first[k], P), :]).then_inc(s_rec[h], 16)

                    halves(e, HALF_T, group)

                @block.vector
                def _(e):
                    def step(last, this, coming):
                        if last:
                            i0, h0 = last
                            g0 = 2 * i0 + h0
                            block16 = tile_values(e, 0, g0 * G, R * (NB - 1))

                        def add_counts(k):
                            if last:
                                e.wait_ge(s_c, g0 + 1)
                                wait(e, s_cadd, g0 * G + k)
                                at = counts[:, bass.ds(block16[k], R)]
                                e.tensor_tensor(at, at, ps_c[:, k, :], ALU.add).then_inc(s_cadd, 1)

                        if coming:
                            i1, h1 = coming
                            g1 = 2 * i1 + h1
                            e.wait_ge(s_rec[h1], (16 * G) * (i1 + 1))
                            wait(e, s_tab, g1 - 1)
                            e.tensor_tensor(here[h1][:, :], rec[h1][:, :, DST], blk_d[:, bass.ds(g1 * G, G)], ALU.subtract).then_inc(s_loc, 1)
                            e.scalar_tensor_tensor(out=kind[h1][:, :], in0=rec[h1][:, :, SRC], scalar=-float(R),
                                                   in1=rec[h1][:, :, ROW], op0=ALU.mult, op1=ALU.add).then_inc(s_typ, 1)
                        add_counts(0)
                        if coming:
                            wait(e, s_c, g1 - 1)
                            e.wait_ge(s_loc, g1 + 1)
                            e.scalar_tensor_tensor(out=skey[h1][:, :], in0=here[h1][:, :], scalar=float(P),
                                                   in1=rec[h1][:, :, SBLK], op0=ALU.is_lt, op1=ALU.mult).then_inc(s_key, 1)
                            e.tensor_tensor(node[h1][:, :, :], over_groups(iota[:, 0:P], P), over_width(here[h1][:, :], P),
                                            ALU.is_equal).then_inc(s_node, 1)
                        add_counts(1)
                        if this:
                            i, h = this
                            g = 2 * i + h
                            wait(e, s_red, g)
                            e.wait_ge(s_before, 2 * g + 1)
                            e.tensor_tensor(rank[:, 0:RG, :], ranks[:, :, :], hot[h][:, 0:RG, :], ALU.mult).then_inc(s_read, 1)
                        add_counts(2)
                        if last:
                            e.wait_ge(s_wp, g0 + 1)
                            e.wait_ge(s_hc, g0 + 1)
                            wait(e, s_msg[h0], i0 * (16 * G))
                            e.tensor_tensor(msg[h0][:, :, 0:P], ps_w[:, :, :], hcut[h0][:, :, :], ALU.mult).then_inc(s_m, 1)
                        add_counts(3)
                        if last:
                            e.wait_ge(s_red, g0 + 1)
                            e.tensor_scalar(pos[h0][:, :], posf[h0][:, :], AHEAD, None, ALU.add).then_inc(s_pos, 1)
                        if this:
                            e.wait_ge(s_before, 2 * g + 2)
                            e.tensor_tensor(rank[:, RG:G, :], ranks[:, :, :], hot[h][:, RG:G, :], ALU.mult).then_inc(s_read, 1)
                        if coming:
                            e.wait_ge(s_key, g1 + 1)
                            wait(e, s_after, 2 * (g1 - 1))
                            e.tensor_tensor(hot[h1][:, :, :], over_groups(iota[:, 1:NB + 1], NB), over_width(skey[h1][:, :], NB),
                                            ALU.is_equal).then_inc(s_hot, 1)
                            e.wait_ge(s_typ, g1 + 1)
                            e.tensor_tensor(hott[h1][:, :, :], over_groups(iota[:, 0:R], R), over_width(kind[h1][:, :], R),
                                            ALU.is_equal).then_inc(s_hott, 1)
                        if this:
                            e.wait_ge(s_read, 2 * g + 2)
                            wait(e, s_pos, g - 1)
                            e.tensor_reduce(posf[h][:, :], rank[:, :, :], AX, ALU.add).then_inc(s_red, 1)
                            e.wait_ge(s_log, g + 1)
                            wait(e, s_wp, g - 1)
                            e.scalar_tensor_tensor(out=filt[h][:, :, :], in0=ps_v[h][:, :].rearrange("p (k n) -> p k n", k=G),
                                                   scalar=0.0, in1=soft[h][:, :].rearrange("p (k n) -> p k n", k=G),
                                                   op0=ALU.max, op1=ALU.add).then_inc(s_filt, 1)

                    e.memset(counts[:, :], 0.0).then_inc(s_set, 1)
                    e.memset(half[:, :], 0.5).then_inc(s_set, 1)
                    e.wait_ge(s_w, 64)
                    for n, (whole, split) in enumerate(((wf1, wparts), (bf2, bparts))):
                        for part in (HIGH, MID):
                            e.tensor_copy(split[:, part, :], whole[:, :]).then_inc(s_parts, 1)
                            e.wait_ge(s_parts, 5 * n + 2 * part + 1)
                            e.tensor_tensor(whole[:, :], whole[:, :], split[:, part, :], ALU.subtract).then_inc(s_parts, 1)
                            e.wait_ge(s_parts, 5 * n + 2 * part + 2)
                        e.tensor_copy(split[:, LOW, :], whole[:, :]).then_inc(s_parts, 1)
                    e.wait_ge(s_set, 2)
                    pipeline(e, HALF_T, step)

                @block.scalar
                def _(e):
                    def step(last, this, coming):
                        if this:
                            i, h = this
                            g = 2 * i + h
                            e.wait_ge(s_vp, g + 1)
                            wait(e, s_filt, g - 1)
                            e.activation(soft[h][:, :], ps_v[h][:, :], ACT.Abs).then_inc(s_abs, 1)
                        if coming:
                            i1, h1 = coming
                            g1 = 2 * i1 + h1
                            wait(e, s_srcs, g1 - 1)
                            wait(e, s_hc, g1 - 1)
                            e.wait_ge(s_rec[h1], (16 * G) * (i1 + 1))
                            e.activation(late[h1][:, :, :], rec[h1][:, :, WORDS:REC], ACT.Copy).then_inc(s_late, 1)
                        if this:
                            e.wait_ge(s_abs, g + 1)
                            e.activation(soft[h][:, :], soft[h][:, :], ACT.Exp, scale=-1.0).then_inc(s_exp, 1)
                        if coming:
                            e.wait_ge(s_fp, g1 + 1)
                            wait(e, s_vp, g1 - 1)
                            e.activation(fT[h1][:, :], ps_f[0:KF, :], ACT.Copy).then_inc(s_fT, 1)
                        if this:
                            e.wait_ge(s_exp, g + 1)
                            e.activation(soft[h][:, :], soft[h][:, :], ACT.Ln, scale=0.5, bias=half[:, 0:1]).then_inc(s_log, 1)
                        if this:
                            e.wait_ge(s_late, g + 1)
                            wait(e, s_src, g - 1)
                            e.activation(srcs[h][:, :, :], late[h][:, :, SRC - WORDS:SRC - WORDS + 1], ACT.Copy)\
                             .then_inc(s_srcs, 1)
                            e.wait_ge(s_g, g + 1)
                            wait(e, s_m, g - 1)
                            for k in range(G):
                                ins = e.activation(hcut[h][:, k, :], ps_g[:, k, :], ACT.Copy,
                                                   scale=late[h][:, k, CUT - WORDS:CUT - WORDS + 1])
                            ins.then_inc(s_hc, 1)
                        if last:
                            i0, h0 = last
                            g0 = 2 * i0 + h0
                            e.wait_ge(s_srcs, g0 + 1)
                            wait(e, s_msg[h0], i0 * (16 * G))
                            e.activation(msg[h0][:, :, P:MSG], srcs[h0][:, :, :], ACT.Copy).then_inc(s_src, 1)
                        if coming:
                            tiles = bass.ds(g1 * G, G)
                            e.wait_ge(s_loc, g1 + 1)
                            e.wait_ge(s_typ, g1 + 1)
                            e.wait_ge(s_late, g1 + 1)
                            settle(e)
                            e.activation(loc[:, tiles], here[h1][:, :], ACT.Copy)
                            e.activation(row[:, tiles], late[h1][:, :, ROW - WORDS], ACT.Copy)
                            e.activation(typ[:, tiles], kind[h1][:, :], ACT.Copy).then_inc(s_tab, 1)
                            e.wait_ge(s_np, g1 + 1)
                            wait(e, s_g, g1 - 1)
                            e.activation(nodeT[h1][:, :, :], ps_n[:, :, :], ACT.Copy).then_inc(s_nT, 1)

                    e.wait_ge(s_set, 2)
                    e.preload_act_table_set("natural_log_exp_and_others")
                    pipeline(e, HALF_T, step)

                @block.tensor
                def _(e):
                    def step(last, this, coming):
                        if this:
                            i, h = this
                            g = 2 * i + h
                            e.wait_ge(s_fT, g + 1)
                            wait(e, s_filt, g - 1)
                            e.matmul(ps_v[h][:, :], wstack[:, :], fT[h][:, :], start=True, stop=True).then_inc(s_vp, 1)
                            e.wait_ge(s_hot, g + 1)
                            rank_before(e, ranks, hot[h], 0).then_inc(s_before, 1)
                        if last:
                            i0, h0 = last
                            g0 = 2 * i0 + h0
                            wait(e, s_m, g0)
                            e.matmul(ps_w[:, :, :], onesb[0:3, :], brows[:, :, :], start=True, stop=False,
                                     skip_group_check=True)
                            e.wait_ge(s_filt, g0 + 1)
                            for k in range(G):
                                mm = e.matmul(ps_w[:, k, :], filt[h0][:, k, :], wf2[:, :], start=False, stop=True,
                                              skip_group_check=True)
                            mm.then_inc(s_wp, 1)
                        if coming:
                            i1, h1 = coming
                            g1 = 2 * i1 + h1
                            e.wait_ge(s_rec[h1], (16 * G) * (i1 + 1))
                            wait(e, s_fT, g1)
                            for k in range(G):
                                mm = e.transpose(ps_f[0:KF, k * P:(k + 1) * P], stacks[h1][:, k, 0:KF], identb[:, :])
                            mm.then_inc(s_fp, 1)
                        if this:
                            block16 = tile_values(e, 0, g * G, R * (NB - 1))
                            e.wait_ge(s_read, 2 * g + 1)
                            rank_after(e, ranks, hot[h], 0).then_inc(s_after, 1)
                            rank_before(e, ranks, hot[h], RG).then_inc(s_before, 1)
                            e.wait_ge(s_nT, g + 1)
                            wait(e, s_hc, g)
                            for k in range(G):
                                for part in range(3):
                                    mm = e.matmul(ps_g[:, k, :], nodeT[h][:, k, :],
                                                  hf_rows[:, bass.ds(block16[k] * (3 * P // R) + part * P, P)],
                                                  start=(part == 0), stop=(part == 2))
                            mm.then_inc(s_g, 1)
                            e.wait_ge(s_read, 2 * g + 2)
                            rank_after(e, ranks, hot[h], RG).then_inc(s_after, 1)
                            e.wait_ge(s_hott, g + 1)
                            wait(e, s_cadd, g * G)
                            for k in range(G):
                                mm = e.matmul(ps_c[:, k, :], node[h][:, k, :], hott[h][:, k, :], start=True, stop=True)
                            mm.then_inc(s_c, 1)
                        if coming:
                            e.wait_ge(s_node, g1 + 1)
                            wait(e, s_nT, g1)
                            for k in range(G):
                                mm = e.transpose(ps_n[:, k, :], node[h1][:, k, :], identb[:, :])
                            mm.then_inc(s_np, 1)

                    hf_rows = hf[:, :, :, :].rearrange("p b t f -> p (b t f)")
                    e.wait_ge(s_w, 64)
                    e.wait_ge(s_stack, 16 * (len(STACK) + 6))
                    rank_start(e, ranks, 1)
                    pipeline(e, HALF_T, step)

                @block.gpsimd
                def _(e):
                    def group(i, h):
                        g = 2 * i + h
                        e.wait_ge(s_m, g + 1)
                        e.wait_ge(s_src, g + 1)
                        e.wait_ge(s_pos, g + 1)
                        settle(e)
                        for k in range(G):
                            e.indirect_dma_start(
                                out=msgs, out_offset=bass.IndirectOffsetOnAxis(ap=pos[h][:, k:k + 1], axis=0),
                                in_=msg[h][:, k, :], in_offset=None, bounds_check=E - 1, oob_is_err=False)\
                             .then_inc(s_msg[h], 16)

                    halves(e, HALF_T, group)
                    for h in range(2):
                        e.wait_ge(s_msg[h], HALF_T * 16 * G)

        acc = sb("acc", [P, (NBP + 1) * P])
        wl = sb("wl", [P, R * P])
        wr = sb("wr", [P, P])
        bl = sb("bl", [P, 1])
        parts = sb("parts", [P, GROUPS, 2], I32)
        behind = sb("behind", [P, 1], I32)

        def add_tile(e, g, k, block16, sums, s_add, acc=acc):
            wait(e, s_add, g * G + k)
            at = acc[:, bass.ds(block16[k] * (P // R), P)]
            e.tensor_tensor(at, at, sums[:, k, :], ALU.add).then_inc(s_add, 1)

        with ExitStack() as c:
            L = 2 * G
            HALF_L = T // (2 * L)
            msg = [sb(f"msg{h}", [P, L, MSG], c=c) for h in range(2)]
            here = [sb(f"here{h}", [P, L], c=c) for h in range(2)]
            nodes = [sb(f"nodes{h}", [P, L, P], c=c) for h in range(2)]
            ps_a = [psum(f"ps_a{h}", [P, L, P], c=c) for h in range(2)]
            s_msg = [sem(f"messages_loaded{h}", c) for h in range(2)]
            s_acc, s_here, s_nodes = sem("sums_cleared", c), sem("local_src", c), sem("src_hot", c)
            s_v = sem("dve_step", c)
            ones = sb("ones", [P, GROUPS], c=c)
            final = sb("final", [P, GROUPS], c=c)
            through = sb("through", [P, GROUPS], c=c)
            parti = sb("parti", [P, GROUPS], I32, c)
            blockf = sb("blockf", [P, GROUPS], c=c)
            spare = sb("spare", [P, GROUPS], c=c)
            s_prod, s_add = sem("sums_ready", c), sem("sums_added", c)

            def load(e, i, h, part):
                g = 2 * i + h
                first = tile_values(e, 96, g * L + part * G, E)
                wait(e, s_prod, 2 * (g - 1) - 1 + part)
                for k in range(G):
                    e.dma_start(msg[h][:, part * G + k, :], msgs[bass.ds(first[k], P), :]).then_inc(s_msg[h], 16)

            with nc.Block() as block:

                @block.sync
                def _(e):
                    halves(e, HALF_L, lambda i, h: load(e, i, h, 0))

                @block.scalar
                def _(e):
                    halves(e, HALF_L, lambda i, h: load(e, i, h, 1))

                @block.vector
                def _(e):
                    def step(last, this, coming):
                        if last:
                            i0, h0 = last
                            g0 = 2 * i0 + h0

                        def add(part):
                            if last:
                                block16 = tile_values(e, 64, g0 * L + part * G, R * (NB - 1))
                                e.wait_ge(s_prod, 2 * g0 + part + 1)
                                for k in range(G):
                                    add_tile(e, 2 * g0 + part, k, block16, ps_a[h0][:, part * G:(part + 1) * G, :], s_add)

                        if this:
                            i, h = this
                            g = 2 * i + h
                            wait(e, s_prod, 2 * (g - 1))
                            e.wait_ge(s_msg[h], (16 * L) * (i + 1))
                            e.tensor_tensor(here[h][:, :], msg[h][:, :, P], blk_s[:, bass.ds(g * L, L)], ALU.subtract)\
                             .then_inc(s_here, 1)
                            e.wait_ge(s_here, g + 1)
                            for part in range(2):
                                tiles = slice(part * G, (part + 1) * G)
                                e.tensor_tensor(nodes[h][:, tiles, :], over_groups(iota[:, 0:P], P),
                                                over_width(here[h][:, tiles], P), ALU.is_equal).then_inc(s_nodes, 1)
                        for part in range(2):
                            add(part)

                    steps = [0]

                    def then_wait(ins):
                        steps[0] += 1
                        ins.then_inc(s_v, 1)
                        e.wait_ge(s_v, steps[0])

                    e.memset(acc[:, :], 0.0).then_inc(s_acc, 1)
                    e.wait_ge(s_acc, 1)
                    e.memset(ones[:, :], 1.0)
                    e.memset(final[:, 0:1], 0.0)
                    then_wait(e.tensor_scalar(final[:, 1:GROUPS],
                                              blk_d[:, :].rearrange("p (g k) -> p g k", k=G)[:, 0:GROUPS - 1, 0],
                                              float(QUARTERS) / P, None, ALU.mult))
                    then_wait(e.tensor_tensor_scan(through[:, :], ones[:, :], final[:, :], 0.0, ALU.add, ALU.min))
                    then_wait(e.tensor_scalar(behind[:, :], through[:, GROUPS - 1:GROUPS], float(QUARTERS * (NB - 1)), None, ALU.is_lt))
                    then_wait(e.tensor_scalar(through[:, :], through[:, :], -1.0, None, ALU.add))
                    then_wait(e.tensor_copy(parti[:, :], through[:, :]))
                    then_wait(e.tensor_scalar(parti[:, :], parti[:, :], 2, None, ALU.arith_shift_right))
                    then_wait(e.tensor_copy(blockf[:, :], parti[:, :]))
                    e.scalar_tensor_tensor(out=parts[:, :, 1], in0=blockf[:, :], scalar=-float(QUARTERS),
                                           in1=through[:, :], op0=ALU.mult, op1=ALU.add)
                    then_wait(e.tensor_scalar(spare[:, :], blockf[:, :], 0.0, float(NB + 1), ALU.is_lt, ALU.mult))
                    then_wait(e.tensor_tensor(parts[:, :, 0], blockf[:, :], spare[:, :], ALU.add))
                    pipeline(e, HALF_L, step)

                @block.tensor
                def _(e):
                    def group(i, h):
                        g = 2 * i + h
                        for part in range(2):
                            e.wait_ge(s_nodes, 2 * g + part + 1)
                            wait(e, s_add, (g - 2) * L + (part + 1) * G)
                            for k in range(part * G, (part + 1) * G):
                                mm = e.matmul(ps_a[h][:, k, :], msg[h][:, k, 0:P], nodes[h][:, k, :], start=True, stop=True)
                            mm.then_inc(s_prod, 1)

                    halves(e, HALF_L, group)

        normed = ExitStack()
        hx = sb("hx", [P, NBP, P], c=normed)
        rstd = sb("rstd", [P, NBP], c=normed)
        with ExitStack() as c:
            NW = G * P
            wo1 = sb("wo1", [P, P], c=c)
            wo2 = sb("wo2", [P, P], c=c)
            bo1 = sb("bo1", [P, 1], c=c)
            bo2 = sb("bo2", [P, P], c=c)
            half = sb("half", [P, 1], c=c)
            var = sb("var", [P, NBP], c=c)
            soft = sb("soft", [P, NW], c=c)
            act = sb("act", [P, NW], c=c)
            xl = [sb(f"xl{h}", [P, G, P], c=c) for h in range(2)]
            x1 = [sb(f"x1_{h}", [P, G, P], c=c) for h in range(2)]
            tot = sb("tot", [P, G], c=c)
            sq = sb("sq", [P, G, P], c=c)
            ps_v = psum("ps_v", [P, NW], c=c)
            ps_o = psum("ps_o", [P, G, P], c=c)
            s_w, s_half = sem("weights_loaded", c), sem("half_set", c)
            s_x = [sem(f"x_loaded{h}", c) for h in range(2)]
            s_st = [sem(f"x1_stored{h}", c) for h in range(2)]
            s_vp, s_abs, s_exp, s_log, s_pos = sem("product1", c), sem("abs", c), sem("exp", c), sem("log", c), sem("positive", c)
            s_act, s_op, s_v, s_x1, s_c = sem("softplus_ready", c), sem("product2", c), sem("dve_step", c), sem("x1_ready", c), sem("centered", c)
            s_sq, s_var, s_std = sem("squared", c), sem("variances_ready", c), sem("std_ready", c)
            with nc.Block() as block:
                NGR = NBP // G

                def normalise(e, n):
                    h = n % 2
                    rows = slice(n * G, (n + 1) * G)
                    e.wait_ge(s_op, n + 1)
                    e.wait_ge(s_x[h], 16 * (n // 2 + 1))
                    wait(e, s_st[h], 16 * (n // 2))
                    e.tensor_tensor(x1[h][:, :, :], ps_o[:, :, :], over_groups(bo2[:, :], P), ALU.add).then_inc(s_v, 1)
                    e.wait_ge(s_v, n + 1)
                    e.tensor_tensor(x1[h][:, :, :], x1[h][:, :, :], xl[h][:, :, :], ALU.add).then_inc(s_x1, 1)
                    e.wait_ge(s_x1, n + 1)
                    e.tensor_reduce(tot[:, :], x1[h][:, :, :], AX, ALU.add).then_inc(s_c, 1)
                    e.wait_ge(s_c, 3 * n + 1)
                    e.tensor_scalar(tot[:, :], tot[:, :], 1.0 / P, None, ALU.mult).then_inc(s_c, 1)
                    e.wait_ge(s_c, 3 * n + 2)
                    e.tensor_tensor(hx[:, rows, :], x1[h][:, :, :], over_width(tot[:, :], P), ALU.subtract).then_inc(s_c, 1)
                    e.wait_ge(s_c, 3 * n + 3)
                    e.tensor_tensor(sq[:, :, :], hx[:, rows, :], hx[:, rows, :], ALU.mult).then_inc(s_sq, 1)
                    e.wait_ge(s_sq, 2 * n + 1)
                    e.tensor_reduce(var[:, rows], sq[:, :, :], AX, ALU.add).then_inc(s_sq, 1)
                    e.wait_ge(s_sq, 2 * n + 2)

                def store(e, n):
                    h = n % 2
                    e.wait_ge(s_x1, n + 1)
                    e.dma_start(x1d[n * NW:(n + 1) * NW, :].rearrange("(k p) f -> p k f", p=P), x1[h][:, :, :])\
                     .then_inc(s_st[h], 16)

                @block.sync
                def _(e):
                    e.dma_start(wo1[:, :], w_o1).then_inc(s_w, 16)
                    e.dma_start(wo2[:, :], w_o2).then_inc(s_w, 16)
                    e.dma_start(bo1[:, :], b_o1.rearrange("(f a) -> f a", a=1)).then_inc(s_w, 16)
                    e.dma_start(bo2[:, :], b_o2.rearrange("(a f) -> a f", a=1).broadcast_to([P, P])).then_inc(s_w, 16)
                    for n in range(NGR):
                        h = n % 2
                        rows = slice(n * NW, (n + 1) * NW)
                        wait(e, s_x1, n - 1)
                        e.dma_start(xl[h][:, :, :], xpad[rows, :].rearrange("(k p) f -> p k f", p=P)).then_inc(s_x[h], 16)
                        if n:
                            store(e, n - 1)
                    store(e, NGR - 1)
                    for h in range(2):
                        e.wait_ge(s_st[h], 16 * ((NGR - h + 1) // 2))

                @block.scalar
                def _(e):
                    e.wait_ge(s_w, 64)
                    e.wait_ge(s_half, 1)
                    for n in range(NGR):
                        e.wait_ge(s_vp, n + 1)
                        wait(e, s_act, n)
                        e.activation(soft[:, :], ps_v[:, :], ACT.Abs, bias=bo1[:, 0:1]).then_inc(s_abs, 1)
                        e.wait_ge(s_abs, n + 1)
                        e.activation(soft[:, :], soft[:, :], ACT.Exp, scale=-1.0).then_inc(s_exp, 1)
                        e.wait_ge(s_exp, n + 1)
                        e.activation(soft[:, :], soft[:, :], ACT.Ln, scale=0.5, bias=half[:, 0:1]).then_inc(s_log, 1)
                    e.wait_ge(s_var, 1)
                    e.activation(var[:, :], var[:, :], ACT.Sqrt).then_inc(s_std, 1)

                @block.tensor
                def _(e):
                    e.wait_ge(s_w, 64)
                    for n in range(NGR + 1):
                        if n < NGR:
                            wait(e, s_pos, n)
                            wait(e, s_abs, n)
                            e.matmul(ps_v[:, :], wo1[:, :], acc[:, n * NW:(n + 1) * NW], start=True, stop=True)\
                             .then_inc(s_vp, 1)
                        if n:
                            e.wait_ge(s_act, n)
                            wait(e, s_v, n - 1)
                            for k in range(G):
                                mm = e.matmul(ps_o[:, k, :], act[:, k * P:(k + 1) * P], wo2[:, :], start=True, stop=True)
                            mm.then_inc(s_op, 1)

                @block.vector
                def _(e):
                    e.memset(half[:, :], 0.5).then_inc(s_half, 1)
                    e.wait_ge(s_w, 64)
                    e.wait_ge(s_half, 1)
                    for n in range(NGR + 1):
                        if n < NGR:
                            e.wait_ge(s_vp, n + 1)
                            e.wait_ge(s_abs, n + 1)
                            wait(e, s_op, n)
                            e.tensor_scalar(act[:, :], ps_v[:, :], bo1[:, 0:1], 0.0, ALU.add, ALU.max).then_inc(s_pos, 1)
                            e.wait_ge(s_pos, n + 1)
                            e.wait_ge(s_log, n + 1)
                            e.tensor_tensor(act[:, :], act[:, :], soft[:, :], ALU.add).then_inc(s_act, 1)
                        if n:
                            normalise(e, n - 1)
                    e.wait_ge(s_sq, 2 * NGR)
                    e.tensor_scalar(var[:, :], var[:, :], 1.0 / P, EPS, ALU.mult, ALU.add).then_inc(s_var, 1)
                    e.wait_ge(s_std, 1)
                    e.reciprocal(rstd[:, :], var[:, :])

        s_st = [sem(f"products_stored{h}") for h in range(2)]
        s_hn, s_tr, s_hT, s_rp, s_root = (sem("h_ready"), sem("h_turned"), sem("hT_ready"),
                                          sem("root_product"), sem("root_added"))
        s_yp, s_yv, s_ya = sem("products_ready"), sem("products_copied_dve"), sem("products_copied_act")
        s_w = sem("layer_weights_loaded")
        accs = [acc]
        s_idx, s_hot, s_prod, s_add = sem("indices_ready"), sem("weighted_hot"), sem("sums_ready"), sem("sums_added")

        products = (*s_st, s_hn, s_tr, s_hT, s_rp, s_root, s_yp, s_yv, s_ya)
        for layer in range(LAYERS):
            T0 = layer * HALF_T
            acc, ytab = accs[layer % 2], ytabs[layer % 2]
            yrows = ytab[0:NB * P, :].rearrange("n (r f) -> (n r) f", r=R)
            with (normed if layer == 0 else ExitStack()), ExitStack() as c:
                hn = [sb(f"hn{h}", [P, P], c=c) for h in range(2)]
                hT = [sb(f"hT{h}", [P, P], c=c) for h in range(2)]
                yst = [sb(f"yst{h}", [P, R * P], c=c) for h in range(2)]
                ps_t = [psum(f"ps_t{h}", [P, P], c=c) for h in range(2)]
                ps_r = [psum(f"ps_r{h}", [P, P], c=c) for h in range(2)]
                ps_y = [psum(f"ps_y{q}", [P, 512], c=c) for q in range(4)]

                def load_weights(e, layer):
                    e.dma_start(wl[:, :].rearrange("i (r o) -> i r o", r=R), w_rel[layer].rearrange("r i o -> i r o"))\
                     .then_inc(s_w, 16)
                    e.dma_start(wr[:, :], w_root[layer]).then_inc(s_w, 16)
                    e.dma_start(bl[:, :], bias_rel[layer].rearrange("(f a) -> f a", a=1)).then_inc(s_w, 16)

                def all_or_last(e, every, last):
                    if layer == 0:
                        every()
                        return
                    left = e.value_load(behind[0:1, 0:1], min_val=0, max_val=1)
                    with e.If(left > 0):
                        every()
                    with e.Else():
                        last()

                with nc.Block() as block:

                    @block.sync
                    def _(e):
                        if layer == 0:
                            load_weights(e, 0)

                        def group(i, h, m=None):
                            n = 2 * i + h
                            m = n if m is None else m
                            e.wait_ge(s_yv, 2 * (n + 1))
                            e.wait_ge(s_ya, 2 * (n + 1))
                            e.dma_start(ytab[bass.ds(m * P, P), :], yst[h][:, :]).then_inc(s_st[h], 16)

                        def every():
                            halves(e, NB // 2, group)
                            for h in range(2):
                                e.wait_ge(s_st[h], 16 * (NB // 2))

                        def last():
                            group(0, 0, NB - 1)
                            e.wait_ge(s_st[0], 16)

                        all_or_last(e, every, last)

                    @block.vector
                    def _(e):
                        def first_half(i, h, m=None):
                            n = 2 * i + h
                            m = n if m is None else m
                            if layer == 0:
                                wait(e, s_tr, n - 1)
                                e.tensor_scalar(hn[h][:, :], hx_rows[:, bass.ds(m * P, P)], rstd[:, bass.ds(m, 1)], None,
                                                ALU.mult).then_inc(s_hn, 1)

                        def second_half(i, h, m=None):
                            n = 2 * i + h
                            m = n if m is None else m
                            wait(e, s_st[h], 16 * i)
                            for q in (0, 2):
                                e.wait_ge(s_yp, 4 * n + q + 1)
                                e.tensor_copy(yst[h][:, q * 512:(q + 1) * 512], ps_y[q][:, :]).then_inc(s_yv, 1)

                        hx_rows = hx[:, :, :].rearrange("p m f -> p (m f)")

                        def every():
                            staggered(e, NB // 2, first_half, second_half)

                        def last():
                            first_half(0, 0, NB - 1)
                            second_half(0, 0, NB - 1)

                        all_or_last(e, every, last)

                    @block.scalar
                    def _(e):
                        def first_half(i, h, m=None):
                            n = 2 * i + h
                            m = n if m is None else m
                            wait(e, s_yp, 4 * (n - 1))
                            if layer == 0:
                                e.wait_ge(s_tr, n + 1)
                                e.activation(hT[h][:, :], ps_t[h][:, :], ACT.Relu).then_inc(s_hT, 1)
                            else:
                                settle(e)
                                e.activation(hT[h][:, :], accs[1 - layer % 2][:, bass.ds(m * P, P)], ACT.Relu).then_inc(s_hT, 1)

                        def second_half(i, h, m=None):
                            n = 2 * i + h
                            m = n if m is None else m
                            e.wait_ge(s_rp, n + 1)
                            e.wait_ge(s_hT, n + 1)
                            settle(e)
                            e.activation(acc[:, bass.ds(m * P, P)], ps_r[h][:, :], ACT.Identity, bias=bl[:, 0:1])\
                             .then_inc(s_root, 1)
                            wait(e, s_st[h], 16 * i)
                            for q in (1, 3):
                                e.wait_ge(s_yp, 4 * n + q + 1)
                                e.activation(yst[h][:, q * 512:(q + 1) * 512], ps_y[q][:, :], ACT.Copy).then_inc(s_ya, 1)

                        e.wait_ge(s_w, 48 * (layer + 1))

                        def every():
                            staggered(e, NB // 2, first_half, second_half)

                        def last():
                            first_half(0, 0, NB - 1)
                            second_half(0, 0, NB - 1)

                        all_or_last(e, every, last)

                    @block.tensor
                    def _(e):
                        def first_half(i, h, m=None):
                            n = 2 * i + h
                            m = n if m is None else m
                            if layer == 0:
                                e.wait_ge(s_hn, n + 1)
                                wait(e, s_hT, n - 1)
                                e.transpose(ps_t[h][:, :], hn[h][:, :], identf[:, :]).then_inc(s_tr, 1)

                        def second_half(i, h, m=None):
                            n = 2 * i + h
                            m = n if m is None else m
                            e.wait_ge(s_hT, n + 1)
                            wait(e, s_root, n - 1)
                            e.matmul(ps_r[h][:, :], wr[:, :], hT[h][:, :], start=True, stop=True).then_inc(s_rp, 1)
                            for q in range(4):
                                wait(e, (s_yv, s_ya)[q % 2], 2 * n - 1 + q // 2)
                                e.matmul(ps_y[q][:, :], hT[h][:, :], wl[:, q * 512:(q + 1) * 512], start=True, stop=True)\
                                 .then_inc(s_yp, 1)

                        e.wait_ge(s_w, 48 * (layer + 1))

                        def every():
                            staggered(e, NB // 2, first_half, second_half)

                        def last():
                            first_half(0, 0, NB - 1)
                            second_half(0, 0, NB - 1)

                        all_or_last(e, every, last)
                clear(products)

            ahead = layer < LAYERS - 1
            with ExitStack() as c:
                if layer == 0:
                    accs.append(sb("acc_odd", [P, (NBP + 1) * P]))
                if ahead:
                    anext, ynext = accs[1 - layer % 2], ytabs[1 - layer % 2]
                    hT = [sb(f"hT{h}", [P, P], c=c) for h in range(2)]
                    yst = [sb(f"yst{h}", [P, 512], c=c) for h in range(2)]
                    ps_y = [psum(f"ps_y{h}", [P, 512], c=c) for h in range(2)]
                    ps_r = [psum(f"ps_r{h}", [P, NR], c=c) for h in range(2)]

                def part_of(e, g):
                    flat = parts[0:1, :, :].rearrange("p g n -> p (g n)")
                    values = []
                    for n, most in enumerate((NB, QUARTERS - 1)):
                        _, (value,) = nc.values_load_multi_w_load_instructions(
                            flat[:, bass.ds(2 * g + n, 1)], engines=[e.engine], min_val=0, max_val=most,
                            skip_runtime_bounds_check_because="the parts are numbered within this range")
                        values.append(value)
                    return values

                idx = [sb(f"idx{h}", [P, G], I32, c) for h in range(2)]
                got = [sb(f"got{h}", [P, G, P], c=c) for h in range(2)]
                hotw = [sb(f"hotw{h}", [P, G, P], c=c) for h in range(2)]
                ps_a = [psum(f"ps_a{h}", [P, G, P], c=c) for h in range(2)]
                s_got = [sem(f"rows_gathered{h}", c) for h in range(2)]
                if layer == 0:
                    inv = counts
                    inv3 = sb("inv3", [P, NB, 3, R], BF16, c)
                    node = [sb(f"node{h}", [P, G, P], BF16, c) for h in range(2)]
                    nodeT = [sb(f"nodeT{h}", [P, G, P], BF16, c) for h in range(2)]
                    hott = [sb(f"hott{h}", [P, G, R], BF16, c) for h in range(2)]
                    pick = sb("pick", [P, G, 3, R], c=c)
                    weight = sb("weight", [P, G], c=c)
                    ps_n = psum("ps_n", [P, G, P], BF16, c)
                    ps_i = psum("ps_i", [P, G, 3, R], c=c)
                    s_v, s_inv, s_node, s_hott = sem("dve_step", c), sem("inverse_ready", c), sem("dst_hot", c), sem("type_hot", c)
                    s_np, s_nT, s_ip, s_pick, s_wgt = (sem("dst_hot_turned", c), sem("dst_hotT_copied", c), sem("inverse_rows", c),
                                                       sem("inverse_picked", c), sem("weights_ready", c))
                    s_kept = sem("weights_kept", c)
                with nc.Block() as block:

                    @block.sync
                    def _(e):
                        def group(i, h):
                            g = 2 * i + h
                            m, quarter = part_of(e, g)
                            e.wait_ge(s_ya, g + 1)
                            settle(e)
                            wait(e, s_st[0], 16 * g)
                            settle(e)
                            e.dma_start(ynext[bass.ds(m * P, P), bass.ds(quarter * 512, 512)], yst[h][:, :]).then_inc(s_st[0], 16)

                        if ahead:
                            load_weights(e, layer + 1)
                            halves(e, HALF_T, group)
                            e.wait_ge(s_st[0], 16 * GROUPS)

                    @block.scalar
                    def _(e):
                        def next_part(i, h):
                            g, n = 2 * i + h, 2 * (T0 + i) + h
                            m, _ = part_of(e, g)
                            wait(e, s_add, (n - 1) * G)
                            wait(e, s_yp, g - 1)
                            settle(e)
                            e.activation(hT[h][:, :], acc[:, bass.ds(m * P, P)], ACT.Relu).then_inc(s_hT, 1)

                        def second(i, h):
                            g = 2 * i + h
                            if not ahead:
                                return
                            if isinstance(g, int) and g == 0:
                                e.wait_ge(s_w, 48 * (layer + 2))
                            m, quarter = part_of(e, g)
                            e.wait_ge(s_yp, g + 1)
                            wait(e, s_st[0], 16 * (g - 1))
                            e.activation(yst[h][:, :], ps_y[h][:, :], ACT.Copy).then_inc(s_ya, 1)
                            wait(e, s_root, g)
                            settle(e)
                            e.activation(anext[:, bass.ds(m * P + quarter * NR, NR)], ps_r[h][:, :], ACT.Identity,
                                         bias=bl[:, 0:1]).then_inc(s_root, 1)

                        def group(i, h):
                            g = 2 * i + h
                            n = 2 * (T0 + i) + h
                            wait(e, s_got[h], (16 * G) * i)
                            settle(e)
                            e.activation(idx[h][:, :], row[:, bass.ds(g * G, G)], ACT.Copy).then_inc(s_idx, 1)
                            if layer == 0:
                                e.wait_ge(s_np, g + 1)
                                wait(e, s_ip, g - 1)
                                e.activation(nodeT[h][:, :, :], ps_n[:, :, :], ACT.Copy).then_inc(s_nT, 1)
                                if not (isinstance(g, int) and g == 0):
                                    keep_weights(g - 1)
                            if ahead:
                                next_part(i, h)

                        def keep_weights(g):
                            e.wait_ge(s_wgt, g + 1)
                            settle(e)
                            e.activation(wgt[:, bass.ds(g * G, G)], weight[:, :], ACT.Copy).then_inc(s_kept, 1)

                        staggered(e, HALF_T, group, second)
                        if layer == 0:
                            keep_weights(2 * HALF_T - 1)

                    @block.gpsimd
                    def _(e):
                        def group(i, h):
                            g = 2 * i + h
                            n = 2 * (T0 + i) + h
                            e.wait_ge(s_idx, n + 1)
                            wait(e, s_prod, n - 1)
                            settle(e)
                            for k in range(G):
                                e.indirect_dma_start(
                                    out=got[h][:, k, :], out_offset=None, in_=yrows,
                                    in_offset=bass.IndirectOffsetOnAxis(ap=idx[h][:, k:k + 1], axis=0),
                                    bounds_check=NB * P * R - 1, oob_is_err=False).then_inc(s_got[h], 16)

                        halves(e, HALF_T, group)

                    @block.vector
                    def _(e):
                        def build(i, h):
                            n = 2 * (T0 + i) + h
                            wait(e, s_prod, n - 1)
                            for k in range(G):
                                tile = bass.ds((2 * i + h) * G + k, 1)
                                ins = e.tensor_scalar(hotw[h][:, k, :], iota[:, 0:P], loc[:, tile], wgt[:, tile],
                                                      ALU.is_equal, ALU.mult)
                            ins.then_inc(s_hot, 1)

                        def add(i, h):
                            n = 2 * (T0 + i) + h
                            e.wait_ge(s_prod, n + 1)
                            block16 = tile_values(e, 0, (2 * i + h) * G, R * (NB - 1))
                            for k in range(G):
                                add_tile(e, n, k, block16, ps_a[h], s_add, acc)

                        def step(last, this, coming):
                            if coming:
                                i1, h1 = coming
                                g1 = 2 * i1 + h1
                                tiles = bass.ds(g1 * G, G)
                                wait(e, s_np, g1 - 1)
                                wait(e, s_hot, g1 - 1)
                                e.tensor_tensor(node[h1][:, :, :], over_groups(iota[:, 0:P], P), over_width(loc[:, tiles], P),
                                                ALU.is_equal).then_inc(s_node, 1)
                                wait(e, s_pick, g1 - 1)
                                e.tensor_tensor(hott[h1][:, :, :], over_groups(iota[:, 0:R], R), over_width(typ[:, tiles], R),
                                                ALU.is_equal).then_inc(s_hott, 1)
                            if this:
                                i, h = this
                                g = 2 * i + h
                                e.wait_ge(s_ip, g + 1)
                                wait(e, s_wgt, g)
                                e.wait_ge(s_hott, g + 1)
                                e.tensor_tensor(pick[:, :, :, :], ps_i[:, :, :, :],
                                                hott[h][:, :, :].unsqueeze(2).broadcast_to([P, G, 3, R]), ALU.mult)\
                                 .then_inc(s_pick, 1)
                                e.wait_ge(s_pick, g + 1)
                                wait(e, s_kept, g)
                                wait(e, s_hot, g)
                                e.tensor_reduce(weight[:, :], pick[:, :, :, :].rearrange("p k t r -> p k (t r)"),
                                                AX, ALU.add).then_inc(s_wgt, 1)
                                wait(e, s_prod, g - 1)
                                e.wait_ge(s_node, g + 1)
                                e.wait_ge(s_wgt, g + 1)
                                e.tensor_tensor(hotw[h][:, :, :], node[h][:, :, :], over_width(weight[:, :], P), ALU.mult)\
                                 .then_inc(s_hot, 1)
                            if last:
                                add(*last)

                        if layer == 0:
                            steps = [0]

                            def then_wait(ins):
                                steps[0] += 1
                                ins.then_inc(s_v, 1)
                                e.wait_ge(s_v, steps[0])

                            then_wait(e.memset(accs[1][:, :], 0.0))
                            then_wait(e.tensor_scalar(inv[:, :], counts[:, :], 1.0, None, ALU.max))
                            then_wait(e.reciprocal(inv[:, :], inv[:, :]))
                            blocks = inv[:, :].rearrange("p (b r) -> p b r", r=R)
                            then_wait(e.tensor_copy(inv3[:, :, 0, :], blocks))
                            then_wait(e.tensor_tensor(blocks, blocks, inv3[:, :, 0, :], ALU.subtract))
                            then_wait(e.tensor_copy(inv3[:, :, 1, :], blocks))
                            e.tensor_tensor(inv3[:, :, 2, :], blocks, inv3[:, :, 1, :], ALU.subtract).then_inc(s_inv, 1)
                            pipeline(e, HALF_T, step)
                        else:
                            staggered(e, HALF_T, build, add)

                    @block.tensor
                    def _(e):
                        def group(i, h):
                            if ahead:
                                next_part(i, h)
                            products(i, h)

                        def next_part(i, h):
                            g = 2 * i + h
                            _, quarter = part_of(e, g)
                            e.wait_ge(s_hT, g + 1)
                            wait(e, s_ya, g - 1)
                            wait(e, s_root, g - 1)
                            e.matmul(ps_r[h][:, :], wr[:, :], hT[h][:, bass.ds(quarter * NR, NR)], start=True, stop=True)
                            e.matmul(ps_y[h][:, :], hT[h][:, :], wl[:, bass.ds(quarter * 512, 512)], start=True, stop=True)\
                             .then_inc(s_yp, 1)

                        def products(i, h):
                            n = 2 * (T0 + i) + h
                            e.wait_ge(s_hot, n + 1)
                            e.wait_ge(s_got[h], (16 * G) * (i + 1))
                            wait(e, s_add, (n - 1) * G)
                            for k in range(G):
                                mm = e.matmul(ps_a[h][:, k, :], got[h][:, k, :], hotw[h][:, k, :], start=True, stop=True)
                            mm.then_inc(s_prod, 1)

                        def step(last, this, coming):
                            if coming:
                                i1, h1 = coming
                                g1 = 2 * i1 + h1
                                e.wait_ge(s_node, g1 + 1)
                                wait(e, s_nT, g1)
                                for k in range(G):
                                    mm = e.transpose(ps_n[:, k, :], node[h1][:, k, :], identb[:, :])
                                mm.then_inc(s_np, 1)
                            if this:
                                next_part(*this)
                            if coming:
                                block16 = tile_values(e, 0, g1 * G, R * (NB - 1))
                                e.wait_ge(s_nT, g1 + 1)
                                wait(e, s_pick, g1)
                                for k in range(G):
                                    mm = e.matmul(ps_i[:, k, :, :].rearrange("p t r -> p (t r)"), nodeT[h1][:, k, :],
                                                  inv_rows[:, bass.ds(block16[k] * 3, 3 * R)], start=True, stop=True)
                                mm.then_inc(s_ip, 1)
                            if this:
                                products(*this)

                        e.wait_ge(s_w, 48 * (layer + 2 if ahead else LAYERS))
                        if layer == 0:
                            inv_rows = inv3[:, :, :, :].rearrange("p b t r -> p (b t r)")
                            e.wait_ge(s_inv, 1)
                            pipeline(e, HALF_T, step)
                        else:
                            halves(e, HALF_T, group)
                if ahead:
                    clear(products)

        with ExitStack() as c:
            x1 = [sb(f"x1_{h}", [P, G, P], c=c) for h in range(2)]
            res = [sb(f"res{h}", [P, G, P], c=c) for h in range(2)]
            ps_t = [psum(f"ps_t{h}", [P, G, P], c=c) for h in range(2)]
            s_x = [sem(f"x1_loaded{h}", c) for h in range(2)]
            s_out = [sem(f"out_stored{h}", c) for h in range(2)]
            s_tr, s_res = sem("sums_turned", c), sem("result_ready", c)
            NGR = NBP // G
            with nc.Block() as block:

                @block.sync
                def _(e):
                    for n in range(NGR + 1):
                        h = n % 2
                        if n < NGR:
                            wait(e, s_res, n - 1)
                            e.dma_start(x1[h][:, :, :], x1d[n * G * P:(n + 1) * G * P, :].rearrange("(k p) f -> p k f", p=P))\
                             .then_inc(s_x[h], 16)
                        if n:
                            g, b = 1 - h, (n - 1) * G
                            e.wait_ge(s_res, n)
                            full = min(G, NB - 1 - b)
                            e.dma_start(out[b * P:(b + full) * P, :].rearrange("(k p) f -> p k f", p=P),
                                        res[g][:, 0:full, :]).then_inc(s_out[g], 16)
                            if full < G:
                                e.dma_start(out[(NB - 1) * P:N, :], res[g][0:LAST, full, :]).then_inc(s_out[g], 16)
                    for h in range(2):
                        extra = (NGR - 1) % 2 == h
                        e.wait_ge(s_out[h], 16 * ((NGR - h + 1) // 2 + extra))

                @block.vector
                def _(e):
                    for n in range(NGR):
                        h = n % 2
                        e.wait_ge(s_tr, n + 1)
                        e.wait_ge(s_x[h], 16 * (n // 2 + 1))
                        wait(e, s_out[h], 16 * (n // 2))
                        e.tensor_tensor(res[h][:, :, :], ps_t[h][:, :, :], x1[h][:, :, :], ALU.add).then_inc(s_res, 1)

                @block.tensor
                def _(e):
                    for n in range(NGR):
                        wait(e, s_res, n - 1)
                        for k in range(G):
                            b = n * G + k
                            mm = e.transpose(ps_t[n % 2][:, k, :], accs[(LAYERS - 1) % 2][:, b * P:(b + 1) * P], identf[:, :])
                        mm.then_inc(s_tr, 1)


_INS = ['x', 'src', 'dst', 'edge_attr_20', 'edge_type_16', 'edge_weight', 'L0_gnn_W_in2f', 'L0_gnn_W_filt1',
        'L0_gnn_b_filt1', 'L0_gnn_W_filt2', 'L0_gnn_b_filt2', 'L0_gnn_W_out1', 'L0_gnn_b_out1', 'L0_gnn_W_out2',
        'L0_gnn_b_out2', 'L1_gnn_W', 'L1_gnn_root', 'L1_gnn_bias']


def kernel(**inputs):
    import numpy as _np
    import concourse.bacc as _bacc
    from concourse import mybir as _mybir
    from concourse.bass_utils import run_bass_kernel_spmd as _run

    nc = _bacc.Bacc("TRN2", target_bir_lowering=False, num_devices=1)
    arrays, args = {}, []
    for name in _INS:
        a = _np.ascontiguousarray(inputs[name])
        arrays[f"in_{name}_dram"] = a
        args.append(nc.dram_tensor(f"in_{name}_dram", a.shape, _mybir.dt.from_np(a.dtype), kind="ExternalInput").ap())
    args.append(nc.dram_tensor("out_0_dram", inputs["x"].shape, _mybir.dt.float32, kind="ExternalOutput").ap())
    gnn_kernel(nc, *args)
    r = _run(nc, [arrays], core_ids=[0])
    return r.results[0]["out_0_dram"]
```
